# Optimizing a Trainium2 kernel written in Bass

```python
import numpy as np
import jax
import jax.numpy as jnp

def _softmax(x, axis=-1):
    return jax.nn.softmax(x, axis=axis)

def _gelu(x):
    return jax.nn.gelu(x, approximate=True)

def _silu(x):
    return jax.nn.silu(x)

def _sigmoid(x):
    return jax.nn.sigmoid(x)

def _layernorm(x, axis=-1, eps=1e-05):
    m = jnp.mean(x, axis=axis, keepdims=True)
    v = jnp.var(x, axis=axis, keepdims=True)
    return (x - m) / jnp.sqrt(v + eps)

def _scatter_add(tgt, idx, src, axis=0):
    return tgt.at[idx].add(src)

def _segment_sum(src, seg, n):
    return jax.ops.segment_sum(src, seg, n)
kernel_name = 'mk_sandwich_d2_jaxref_r8_b287c2'

def setup_inputs(seed: int=0):
    np.random.seed(seed)
    _w = jnp.asarray

    def _L0_attn_setup():
        import jax, jax.numpy as jnp
        import numpy as np

        def _rope_tables(T, d):
            half = d // 2
            i = jnp.arange(half, dtype=jnp.float32)
            theta = 10000.0 ** (-2.0 * i / d)
            m = jnp.arange(T, dtype=jnp.float32)[:, None]
            ang = m * theta[None, :]
            return (jnp.cos(ang), jnp.sin(ang))

        def _rotate(v, cos, sin):
            B, T, d = v.shape
            half = d // 2
            v2 = v.reshape(B, T, half, 2)
            even, odd = (v2[..., 0], v2[..., 1])
            c = cos[None, :, :]
            s = sin[None, :, :]
            new_even = even * c - odd * s
            new_odd = even * s + odd * c
            return jnp.stack([new_even, new_odd], axis=-1).reshape(B, T, d)
        key = jax.random.key(seed)
        k1, k2, k3, k4 = jax.random.split(key, 4)
        B, T, d = (4, 256, 128)
        x = jax.random.normal(k1, (B, T, d), dtype=jnp.float32)
        scale = 0.02
        Wq = jax.random.normal(k2, (d, d), dtype=jnp.float32) * scale
        Wk = jax.random.normal(k3, (d, d), dtype=jnp.float32) * scale
        Wv = jax.random.normal(k4, (d, d), dtype=jnp.float32) * scale
        return {'x': x, 'Wq': Wq, 'Wk': Wk, 'Wv': Wv}
    _L0_attn_in = _L0_attn_setup()

    def _L0_ffn_setup():
        import jax, jax.numpy as jnp
        import numpy as np
        D_IN, D_HID = (128, 512)

        def _ternary(key, shape):
            return jax.random.randint(key, shape, -1, 2).astype(jnp.float32)

        def _tlin(x, w, s):
            return jnp.einsum('bsi,oi->bso', x, w) * s
        key = jax.random.key(seed)
        ks = jax.random.split(key, 12)
        inv = lambda fan: 1.0 / np.sqrt(fan).astype(np.float32)
        return {'x': jax.random.normal(ks[0], (4, 256, D_IN), dtype=jnp.float32), 'w1_w': _ternary(ks[1], (D_HID, D_IN)), 'w1_s': jax.random.uniform(ks[2], (D_HID,), dtype=jnp.float32) * inv(D_IN), 'w2_w': _ternary(ks[3], (D_HID, D_IN)), 'w2_s': jax.random.uniform(ks[4], (D_HID,), dtype=jnp.float32) * inv(D_IN), 'h1_w': _ternary(ks[5], (D_HID, D_HID)), 'h1_s': jax.random.uniform(ks[6], (D_HID,), dtype=jnp.float32) * inv(D_HID), 'h2_w': _ternary(ks[7], (D_HID, D_HID)), 'h2_s': jax.random.uniform(ks[8], (D_HID,), dtype=jnp.float32) * inv(D_HID), 'w3_w': _ternary(ks[9], (D_IN, D_HID)), 'w3_s': jax.random.uniform(ks[10], (D_IN,), dtype=jnp.float32) * inv(D_HID)}
    _L0_ffn_in = _L0_ffn_setup()

    def _L1_attn_setup():
        import jax, jax.numpy as jnp
        import numpy as np
        H = 8
        DIM = 128
        DH = DIM // H // 2
        B, N = (2, 256)
        LAMBDA_INIT = 0.5
        COS_MIN, COS_MAX = (0.0, 15.0)
        ALPHA = 0.5
        COS_EPS = 1e-06
        RMS_EPS = 1e-05
        RAW_INIT = float(np.log(1.0 / 15.0 / (1.0 - 1.0 / 15.0)))

        def _l2norm(t):
            return t / jnp.maximum(jnp.linalg.norm(t, axis=-1, keepdims=True), COS_EPS)
        key = jax.random.key(seed)
        ks = jax.random.split(key, 10)
        s = 1.0 / np.sqrt(DIM)
        return {'x': jax.random.normal(ks[0], (B, N, DIM), jnp.float32), 'Wq': jax.random.normal(ks[1], (DIM, DIM), jnp.float32) * s, 'Wk': jax.random.normal(ks[2], (DIM, DIM), jnp.float32) * s, 'Wv': jax.random.normal(ks[3], (DIM, DIM), jnp.float32) * s, 'Wo': jax.random.normal(ks[4], (DIM, DIM), jnp.float32) * s, 'bo': jnp.zeros((DIM,), jnp.float32), 'lambda_q1': jax.random.normal(ks[5], (DH,), jnp.float32) * 0.1, 'lambda_k1': jax.random.normal(ks[6], (DH,), jnp.float32) * 0.1, 'lambda_q2': jax.random.normal(ks[7], (DH,), jnp.float32) * 0.1, 'lambda_k2': jax.random.normal(ks[8], (DH,), jnp.float32) * 0.1, 'delta_gain': jax.random.normal(ks[9], (H,), jnp.float32) * 0.1, 'cos_head_delta': jnp.zeros((H,), jnp.float32), 'cos_logit_scale_raw': jnp.float32(RAW_INIT), 'subln_weight': jnp.ones((2 * DH,), jnp.float32)}
    _L1_attn_in = _L1_attn_setup()

    def _L1_ffn_setup():
        import jax, jax.numpy as jnp
        import numpy as np
        import math
        GOLDEN_CENTER = 1.0 / math.e
        GOLDEN_LOWER = 0.5 - math.log(4.0 / 3.0)
        GOLDEN_UPPER = 0.5
        B, T, D = (4, 256, 128)
        E = 8
        I = 512 // (E // 2)

        def _routing_weights(x, Wr, temperature):
            inh = jax.nn.sigmoid(x @ Wr / temperature)
            in_zone = (inh >= GOLDEN_LOWER) & (inh <= GOLDEN_UPPER)
            dist = jnp.abs(inh - GOLDEN_CENTER)
            w = jnp.exp(-dist / 0.1) * in_zone.astype(x.dtype)
            wsum = w.sum(axis=-1, keepdims=True)
            no_expert = wsum < 1e-08
            fb = jnp.exp(-dist / 0.3)
            _, top2 = jax.lax.top_k(fb, 2)
            fb_mask = jax.nn.one_hot(top2, E, dtype=x.dtype).sum(axis=-2)
            fb_w = fb * fb_mask
            fb_w = fb_w / jnp.clip(fb_w.sum(axis=-1, keepdims=True), 1e-08)
            w = jnp.where(no_expert, fb_w, w)
            wsum = w.sum(axis=-1, keepdims=True)
            return w / jnp.clip(wsum, 1e-08)
        key = jax.random.key(seed)
        k = jax.random.split(key, 6)
        s_d = 1.0 / math.sqrt(D)
        s_i = 1.0 / math.sqrt(I)
        return {'x': jax.random.normal(k[0], (B, T, D), jnp.float32), 'Wg': jax.random.normal(k[1], (E, D, I), jnp.float32) * s_d, 'Wu': jax.random.normal(k[2], (E, D, I), jnp.float32) * s_d, 'Wd': jax.random.normal(k[3], (E, I, D), jnp.float32) * s_i, 'Wr': jax.random.normal(k[4], (D, E), jnp.float32) * s_d, 'temperature': jnp.ones((1,), jnp.float32)}
    _L1_ffn_in = _L1_ffn_setup()
    _d = {'L0_attn_x': _L0_attn_in['x'], 'L0_attn_Wq': _L0_attn_in['Wq'], 'L0_attn_Wk': _L0_attn_in['Wk'], 'L0_attn_Wv': _L0_attn_in['Wv'], 'L0_ffn_w1_w': _L0_ffn_in['w1_w'], 'L0_ffn_w1_s': _L0_ffn_in['w1_s'], 'L0_ffn_w2_w': _L0_ffn_in['w2_w'], 'L0_ffn_w2_s': _L0_ffn_in['w2_s'], 'L0_ffn_h1_w': _L0_ffn_in['h1_w'], 'L0_ffn_h1_s': _L0_ffn_in['h1_s'], 'L0_ffn_h2_w': _L0_ffn_in['h2_w'], 'L0_ffn_h2_s': _L0_ffn_in['h2_s'], 'L0_ffn_w3_w': _L0_ffn_in['w3_w'], 'L0_ffn_w3_s': _L0_ffn_in['w3_s'], 'L1_attn_Wq': _L1_attn_in['Wq'], 'L1_attn_Wk': _L1_attn_in['Wk'], 'L1_attn_Wv': _L1_attn_in['Wv'], 'L1_attn_Wo': _L1_attn_in['Wo'], 'L1_attn_bo': _L1_attn_in['bo'], 'L1_attn_lambda_q1': _L1_attn_in['lambda_q1'], 'L1_attn_lambda_k1': _L1_attn_in['lambda_k1'], 'L1_attn_lambda_q2': _L1_attn_in['lambda_q2'], 'L1_attn_lambda_k2': _L1_attn_in['lambda_k2'], 'L1_attn_delta_gain': _L1_attn_in['delta_gain'], 'L1_attn_cos_head_delta': _L1_attn_in['cos_head_delta'], 'L1_attn_cos_logit_scale_raw': _L1_attn_in['cos_logit_scale_raw'], 'L1_attn_subln_weight': _L1_attn_in['subln_weight'], 'L1_ffn_Wg': _L1_ffn_in['Wg'], 'L1_ffn_Wu': _L1_ffn_in['Wu'], 'L1_ffn_Wd': _L1_ffn_in['Wd'], 'L1_ffn_Wr': _L1_ffn_in['Wr'], 'L1_ffn_temperature': _L1_ffn_in['temperature']}
    _x0 = _d['L0_attn_x']
    _d['L0_attn_x'] = jax.random.normal(jax.random.fold_in(jax.random.key(seed), 1), (2, 1024, 128), dtype=_x0.dtype)
    del _x0
    return _d

def reference(L0_attn_x, L0_attn_Wq, L0_attn_Wk, L0_attn_Wv, L0_ffn_w1_w, L0_ffn_w1_s, L0_ffn_w2_w, L0_ffn_w2_s, L0_ffn_h1_w, L0_ffn_h1_s, L0_ffn_h2_w, L0_ffn_h2_s, L0_ffn_w3_w, L0_ffn_w3_s, L1_attn_Wq, L1_attn_Wk, L1_attn_Wv, L1_attn_Wo, L1_attn_bo, L1_attn_lambda_q1, L1_attn_lambda_k1, L1_attn_lambda_q2, L1_attn_lambda_k2, L1_attn_delta_gain, L1_attn_cos_head_delta, L1_attn_cos_logit_scale_raw, L1_attn_subln_weight, L1_ffn_Wg, L1_ffn_Wu, L1_ffn_Wd, L1_ffn_Wr, L1_ffn_temperature):

    def _L0_attn_ref(x, Wq, Wk, Wv):
        import jax, jax.numpy as jnp
        import numpy as np

        def _rope_tables(T, d):
            half = d // 2
            i = jnp.arange(half, dtype=jnp.float32)
            theta = 10000.0 ** (-2.0 * i / d)
            m = jnp.arange(T, dtype=jnp.float32)[:, None]
            ang = m * theta[None, :]
            return (jnp.cos(ang), jnp.sin(ang))

        def _rotate(v, cos, sin):
            B, T, d = v.shape
            half = d // 2
            v2 = v.reshape(B, T, half, 2)
            even, odd = (v2[..., 0], v2[..., 1])
            c = cos[None, :, :]
            s = sin[None, :, :]
            new_even = even * c - odd * s
            new_odd = even * s + odd * c
            return jnp.stack([new_even, new_odd], axis=-1).reshape(B, T, d)
        B, T, d = x.shape
        cos, sin = _rope_tables(T, d)
        Q = jnp.einsum('btd,ed->bte', x, Wq)
        K = jnp.einsum('btd,ed->bte', x, Wk)
        V = jnp.einsum('btd,ed->bte', x, Wv)
        Qr = _rotate(Q, cos, sin)
        Kr = _rotate(K, cos, sin)
        scores = jnp.einsum('bqd,bkd->bqk', Qr, Kr) / jnp.sqrt(jnp.float32(d))
        mask = jnp.tril(jnp.ones((T, T), dtype=bool), k=1)
        scores = jnp.where(mask[None, :, :], scores, -jnp.inf)
        attn = jax.nn.softmax(scores, axis=-1)
        out = jnp.einsum('bqk,bkd->bqd', attn, V)
        return out

    def _L0_ffn_ref(x, w1_w, w1_s, w2_w, w2_s, h1_w, h1_s, h2_w, h2_s, w3_w, w3_s):
        import jax, jax.numpy as jnp
        import numpy as np
        D_IN, D_HID = (128, 512)

        def _ternary(key, shape):
            return jax.random.randint(key, shape, -1, 2).astype(jnp.float32)

        def _tlin(x, w, s):
            return jnp.einsum('bsi,oi->bso', x, w) * s
        h = jax.nn.silu(_tlin(x, w1_w, w1_s)) * _tlin(x, w2_w, w2_s)
        h = jax.nn.gelu(_tlin(h, h1_w, h1_s), approximate=False)
        h = jax.nn.gelu(_tlin(h, h2_w, h2_s), approximate=False)
        return _tlin(h, w3_w, w3_s)

    def _L1_attn_ref(x, Wq, Wk, Wv, Wo, bo, lambda_q1, lambda_k1, lambda_q2, lambda_k2, delta_gain, cos_head_delta, cos_logit_scale_raw, subln_weight):
        import jax, jax.numpy as jnp
        import numpy as np
        H = 8
        DIM = 128
        DH = DIM // H // 2
        B, N = (2, 256)
        LAMBDA_INIT = 0.5
        COS_MIN, COS_MAX = (0.0, 15.0)
        ALPHA = 0.5
        COS_EPS = 1e-06
        RMS_EPS = 1e-05
        RAW_INIT = float(np.log(1.0 / 15.0 / (1.0 - 1.0 / 15.0)))

        def _l2norm(t):
            return t / jnp.maximum(jnp.linalg.norm(t, axis=-1, keepdims=True), COS_EPS)
        b, n, c = x.shape
        q = (x @ Wq.T).reshape(b, n, H, 2, DH).transpose(0, 2, 3, 1, 4)
        k = (x @ Wk.T).reshape(b, n, H, 2, DH).transpose(0, 2, 3, 1, 4)
        v = (x @ Wv.T).reshape(b, n, H, 2 * DH).transpose(0, 2, 1, 3)
        q1, q2 = (q[:, :, 0], q[:, :, 1])
        k1, k2 = (k[:, :, 0], k[:, :, 1])
        gscale = COS_MIN + (COS_MAX - COS_MIN) * jax.nn.sigmoid(cos_logit_scale_raw)
        head_delta = cos_head_delta - cos_head_delta.mean()
        cos_scale = (gscale * (1.0 + ALPHA * jnp.tanh(head_delta))).reshape(1, H, 1, 1)
        L1 = jnp.einsum('bhnd,bhmd->bhnm', _l2norm(q1), _l2norm(k1)) * cos_scale
        L2 = jnp.einsum('bhnd,bhmd->bhnm', _l2norm(q2), _l2norm(k2)) * cos_scale
        L1 = jnp.nan_to_num(L1)
        L2 = jnp.nan_to_num(L2)
        G = jnp.tanh(delta_gain.reshape(1, H, 1, 1) * (L1 - L2))
        A1 = jax.nn.softmax((L1 + G).astype(jnp.float32), axis=-1).astype(x.dtype)
        A2 = jax.nn.softmax((L2 - G).astype(jnp.float32), axis=-1).astype(x.dtype)
        lambda_1 = jnp.exp(jnp.sum(lambda_q1 * lambda_k1))
        lambda_2 = jnp.exp(jnp.sum(lambda_q2 * lambda_k2))
        lambda_full = (lambda_1 - lambda_2 + LAMBDA_INIT).astype(x.dtype)
        attn = A1 - lambda_full * A2
        y = jnp.einsum('bhnm,bhmd->bhnd', attn, v)
        y = y * jax.lax.rsqrt(jnp.mean(y * y, axis=-1, keepdims=True) + RMS_EPS) * subln_weight
        y = y * (1.0 - LAMBDA_INIT)
        y = y.transpose(0, 2, 1, 3).reshape(b, n, c)
        return y @ Wo.T + bo

    def _L1_ffn_ref(x, Wg, Wu, Wd, Wr, temperature):
        import jax, jax.numpy as jnp
        import numpy as np
        import math
        GOLDEN_CENTER = 1.0 / math.e
        GOLDEN_LOWER = 0.5 - math.log(4.0 / 3.0)
        GOLDEN_UPPER = 0.5
        B, T, D = (4, 256, 128)
        E = 8
        I = 512 // (E // 2)

        def _routing_weights(x, Wr, temperature):
            inh = jax.nn.sigmoid(x @ Wr / temperature)
            in_zone = (inh >= GOLDEN_LOWER) & (inh <= GOLDEN_UPPER)
            dist = jnp.abs(inh - GOLDEN_CENTER)
            w = jnp.exp(-dist / 0.1) * in_zone.astype(x.dtype)
            wsum = w.sum(axis=-1, keepdims=True)
            no_expert = wsum < 1e-08
            fb = jnp.exp(-dist / 0.3)
            _, top2 = jax.lax.top_k(fb, 2)
            fb_mask = jax.nn.one_hot(top2, E, dtype=x.dtype).sum(axis=-2)
            fb_w = fb * fb_mask
            fb_w = fb_w / jnp.clip(fb_w.sum(axis=-1, keepdims=True), 1e-08)
            w = jnp.where(no_expert, fb_w, w)
            wsum = w.sum(axis=-1, keepdims=True)
            return w / jnp.clip(wsum, 1e-08)
        weights = _routing_weights(x, Wr, temperature)
        gate = jnp.einsum('btd,edi->beti', x, Wg)
        up = jnp.einsum('btd,edi->beti', x, Wu)
        h = jax.nn.silu(gate) * up
        e_out = jnp.einsum('beti,eid->betd', h, Wd)
        out = jnp.einsum('bte,betd->btd', weights, e_out)
        return out
    x = L0_attn_x
    x = x + _layernorm(_L0_attn_ref(_layernorm(x, axis=-1), L0_attn_Wq, L0_attn_Wk, L0_attn_Wv), axis=-1)
    x = x + _layernorm(_L0_ffn_ref(_layernorm(x, axis=-1), L0_ffn_w1_w, L0_ffn_w1_s, L0_ffn_w2_w, L0_ffn_w2_s, L0_ffn_h1_w, L0_ffn_h1_s, L0_ffn_h2_w, L0_ffn_h2_s, L0_ffn_w3_w, L0_ffn_w3_s), axis=-1)
    x = x + _layernorm(_L1_attn_ref(_layernorm(x, axis=-1), L1_attn_Wq, L1_attn_Wk, L1_attn_Wv, L1_attn_Wo, L1_attn_bo, L1_attn_lambda_q1, L1_attn_lambda_k1, L1_attn_lambda_q2, L1_attn_lambda_k2, L1_attn_delta_gain, L1_attn_cos_head_delta, L1_attn_cos_logit_scale_raw, L1_attn_subln_weight), axis=-1)
    x = x + _layernorm(_L1_ffn_ref(_layernorm(x, axis=-1), L1_ffn_Wg, L1_ffn_Wu, L1_ffn_Wd, L1_ffn_Wr, L1_ffn_temperature), axis=-1)
    return x

_drawn_inputs = setup_inputs


def setup_inputs(seed=0):
    import zlib

    import numpy as np

    out = dict(_drawn_inputs(seed))
    spreads = {'L1_attn_bo': (0.0, 0.1),
     'L1_attn_cos_head_delta': (0.0, 0.438),
     'L1_attn_subln_weight': (1.0, 0.2)}
    factors = {'L1_attn_lambda_q1': 3.187}
    for name, (base, spread) in spreads.items():
        noise = np.random.default_rng([zlib.crc32(name.encode()), seed]).standard_normal(out[name].shape)
        drawn = base * np.exp(spread * noise) if base else spread * noise
        out[name] = jnp.asarray(drawn.astype(out[name].dtype))
    for name, factor in factors.items():
        out[name] = (out[name] * factor).astype(out[name].dtype)
    return out
```

```python
from contextlib import ExitStack

import numpy as np

import concourse.bass as bass
from concourse import mybir

F32 = mybir.dt.float32
BF16 = mybir.dt.bfloat16
I32 = mybir.dt.int32
ALU = mybir.AluOpType
ACT = mybir.ActivationFunctionType
AX = mybir.AxisListType

P = 128
BATCH, SEQ = 2, 1024
TILES = BATCH * SEQ // P
BT = SEQ // P
CT = 4
CHUNK = CT * P
CHUNKS = TILES // CT
HID = 512
KT_ = HID // P
HEADS, DH = 8, 8
VH = 2 * DH
VW = 32
PARTS = 6
EXPERTS = 8
LN_EPS = 1e-5
RMS_EPS = 1e-5
ATT_SCALE = float(P) ** -0.5
MASKED = -1e30
RSQRT_MAGIC = float(0x5F3759DF)
GOLDEN = float(1.0 / np.e)
ZONE_LOW = float(np.float32(0.5 - np.log(4.0 / 3.0)))
ZONE_HIGH = 0.5
COS_MAX = 15.0
LAMBDA_INIT = 0.5

SM_LAM, SM_GAIN, SM_DELTA, SM_RAW, SM_TEMP, SM_SUBLN, SM_HALF = 0, 32, 40, 48, 49, 50, 51
SM_W = 53
BANK_TURN = 7


class Turn:

    def __init__(self, eng, sem, start=0):
        self.eng, self.sem, self.n = eng, sem, start

    def mark(self, ins):
        self.n += 1
        ins.then_inc(self.sem, 1)

    def wait(self):
        self.eng.wait_ge(self.sem, self.n)

    def step(self, ins):
        self.mark(ins)
        self.wait()


def sandwich(nc, x_in, a_w, rope, b_w12, b_h1, b_h2, b_w3, b_s, b_s3, c_w, c_wo, c_bo, small,
             d_wg, d_wu, d_wd, d_wr, ident_in, ident_bf_in, mask_in, before_in, out):
    with ExitStack() as ctx:
        def sb(name, shape, dt=F32):
            return ctx.enter_context(nc.sbuf_tensor(name, shape, dt))

        def sem(name):
            return ctx.enter_context(nc.semaphore(name))

        x = sb("x_res", [P, TILES, P])
        xn = sb("xn", [P, CT, P])
        xn_c = sb("xn_c", [P, CT, P])
        xt = sb("xt", [P, CHUNK])
        xt_c = sb("xt_c", [P, CHUNK])
        y = sb("y", [P, CT, P])
        ident = sb("ident", [P, P])
        ident_bf = sb("ident_bf", [P, P], BF16)
        mask = sb("mask", [P, P + 1], BF16)
        before = sb("before", [P, CT, EXPERTS, EXPERTS])
        st = sb("st", [P, CT, 6])
        mv = sb("mv", [P, CT, 2])
        nv = sb("nv", [P, P])
        nh = sb("nh", [P, P])
        nt = sb("nt", [P, P])
        rstd = sb("rstd", [P, P])
        w_a = sb("w_a", [P, 5, P])
        tab = sb("tab", [P, 2, SEQ])
        qkv_a = sb("qkv_a", [P, 3, BATCH * SEQ])
        q_t = qkv_a[:, 0].rearrange("p (b s) -> p b s", b=BATCH)
        k_t = qkv_a[:, 1].rearrange("p (b s) -> p b s", b=BATCH)
        v_a = qkv_a[:, 2].rearrange("p (t d) -> p t d", t=TILES)
        rot = sb("rot", [P, 2, CHUNK])
        mx = sb("mx", [P, TILES])
        nmx = sb("nmx", [P, TILES])
        rsum = sb("rsum", [P, TILES])
        rinv = sb("rinv", [P, TILES])
        probs = sb("probs", [P, 2, SEQ])
        probs_t = sb("probs_t", [P, 2, SEQ])
        y_a = sb("y_a", [P, BATCH * BT, P])
        w_12 = sb("w_12", [P, 2, HID])
        w_hh = sb("w_hh", [P, 2, KT_, HID])
        w_h1, w_h2 = w_hh[:, 0], w_hh[:, 1]
        w_3 = sb("w_3", [P, KT_, P])
        s_b = sb("s_b", [P, 16])
        s_3 = sb("s_3", [P, P])
        sg = rot
        hid = sb("hid", [P, 3, KT_, CHUNK])
        w_c = sb("w_c", [P, 3 * P])
        w_o = sb("w_o", [P, P])
        w_os = sb("w_os", [P, P])
        b_o = sb("b_o", [P, P])
        sm = sb("sm", [P, SM_W])
        tiny = sb("tiny", [P, 64])
        nlam = sb("nlam", [P, 1])
        cs_tab = sb("cs_tab", [P, 2, HEADS, CT, 2])
        raw = sb("raw", [P, 2, HEADS, CT * VH])
        sq = sb("sq", [P, 2, HEADS, CT * VH])
        ss = sb("ss", [P, P])
        part = [sb(f"part{i}", [P, 2, BATCH * HEADS, BT * VH], BF16) for i in range(3)]
        v_c = sb("v_c", [P, BATCH * HEADS, BT, VH])
        u_q = sb("u_q", [P, 2, BT, P], BF16)
        u_k = sb("u_k", [P, 2, BT, P], BF16)
        q_s = sb("q_s", [P, 2, SEQ], BF16)
        k_s = sb("k_s", [P, 2, SEQ], BF16)
        k_1 = sb("k_1", [P, 2, SEQ], BF16)
        k_2 = sb("k_2", [P, 2, SEQ], BF16)
        v_h = sb("v_h", [P, 2, BT, VW])
        gain = sb("gain", [P, 2])
        gg = probs
        flat_hid = hid[:].rearrange("p a b c -> p (a b c)")
        zz = flat_hid[:, 0:4 * SEQ].rearrange("p (a b) -> p a b", a=2)
        ee = w_hh[:].rearrange("p a b c -> p (a b c)").rearrange("p (a b) -> p a b", a=2)
        acc_sb = w_12[:, 0]
        o_all = qkv_a[:].rearrange("p a b -> p (a b)")[:, 0:BATCH * HEADS * CT * 4 * (VH + 1)].rearrange(
            "p (n c g v) -> p n c g v", n=BATCH * HEADS, c=CT, g=4)
        r_o = sb("r_o", [P, 2, HEADS * CT])
        t_o = probs_t[:, 1].rearrange("p (a n v) -> p a n v", a=2, v=VH)
        y_c = xn_c
        y_ct = w_12[:, 1]
        w_g = tab[:, 0].rearrange("p (e i) -> p e i", e=EXPERTS)
        w_u = tab[:, 1].rearrange("p (e i) -> p e i", e=EXPERTS)
        w_d = probs_t[:, 0].rearrange("p (e i) -> p e i", e=EXPERTS)
        w_r = sb("w_r", [P, EXPERTS])
        rt = sb("rt", [P, 8, CT, EXPERTS])
        pair = sb("pair", [P, 2, CT, EXPERTS, EXPERTS])
        rs1 = sb("rs1", [P, 4, CT])
        wts = sb("wts", [P, 2, CT, EXPERTS])
        sg_d, h_d = (flat_hid[:, 2 * CHUNK * i:2 * CHUNK * (i + 1)].rearrange("p (a b) -> p a b", a=2)
                     for i in range(2))
        e_out = flat_hid[:, 4 * CHUNK:6 * CHUNK].rearrange("p (a b c) -> p a b c", a=2, b=CT)
        gains = sb("gains", [P, BATCH * HEADS])

        ps = ctx.enter_context(nc.psum_tensor("ps", [P, 8, CHUNK], F32))
        turn = ps[:, BANK_TURN, :]
        turn_bf = turn.bitcast(BF16)

        ld = {n: sem(f"ld_{n}") for n in ("x0", "x1", "x2", "x3", "aw", "tab", "idf", "con", "bw", "bh", "cw", "dw")}
        s_self = {n: sem(f"self_{n}") for n in ("dve", "pool", "act")}
        names = """xn_a tp_a xt_a used_a qp_a kp_a v_a rq1 rk1 rq2 rk2 ropeq ropek vout
            s_a m_a e_a pt_a pe_a o_a y_a
            xn_b tp_b xt_b gu_b sg_b h_b m1_b g1_b m2_b g2_b y_b yo_b
            xn_c tp_c xt_c qkv_c raw_c sq_c qh_c hi_c r1_c mid_c lo_c vraw_c const_c zero_c
            uq uk vh gcp tq tk qs ks k12 dd l1 l2 g z1 z2 e av accout to oo
            yc ytp yt wo xn_d tp_d xt_d rt_d rcopy tanh_d dist_d ex_d w_d gu_d sg_d h_d eo_d sc_d ad_d xfin
            stored""".split()
        S = {n: sem("e_" + n) for n in names}

        block = ctx.enter_context(nc.Block())

        x_src = x_in.rearrange("b (j p) d -> p (b j) d", p=P)
        out_dst = out.rearrange("b (j p) d -> p (b j) d", p=P)

        def chunk(c):
            return slice(c * CT, c * CT + CT)

        def d_xt(c):
            return (xt if c % 2 == 0 else xt_c)[:]

        def y_d(c):
            return y_a[:, (c % 2) * CT:(c % 2) * CT + CT, :]

        def c_table(dve, v, me):
            dve.wait_ge(S["const_c"], 2)
            me.step(v.tensor_tensor(tiny[:, 48:49], tiny[:, 1:2], tiny[:, 0:1], ALU.subtract))
            me.mark(v.tensor_scalar(nlam[:], tiny[:, 48:49], -LAMBDA_INIT, None, ALU.add))
            me.mark(v.tensor_scalar(tiny[:, 49:50], tiny[:, 16:17], COS_MAX / 2, COS_MAX / 2, ALU.mult, ALU.add))
            me.step(v.tensor_scalar(tiny[:, 8:16], tiny[:, 8:16], 0.5, 1.0, ALU.mult, ALU.add))
            me.step(v.tensor_scalar(tiny[:, 8:16], tiny[:, 8:16], tiny[:, 49:50], None, ALU.mult))
            me.mark(v.tensor_copy(cs_tab[:, 0].rearrange("p h k c -> p h (k c)"),
                                  tiny[:, 8:16].unsqueeze(2).to_broadcast([P, HEADS, 2 * CT])))
            me.mark(v.memset(cs_tab[:, 1, :, :, 0], 1.0))
            me.step(v.memset(cs_tab[:, 1, :, :, 1], -1.0))

        @block.sync
        def _(sp):
            for c in range(CHUNKS):
                sp.dma_start(x[:, chunk(c), :], x_src[:, chunk(c), :]).then_inc(ld[f"x{c}"], 16)
                if c == 0:
                    sp.dma_start(ident[:], ident_in).then_inc(ld["idf"], 16)
                    sp.dma_start(w_a[:].rearrange("p a b -> p (a b)"), a_w).then_inc(ld["aw"], 16)
                    sp.dma_start(tab[:], rope).then_inc(ld["tab"], 16)
            sp.dma_start(ident_bf[:], ident_bf_in).then_inc(ld["con"], 16)
            sp.dma_start(mask[:], mask_in).then_inc(ld["con"], 16)
            sp.dma_start(w_12[:].rearrange("p a b -> p (a b)"), b_w12).then_inc(ld["bw"], 16)
            sp.dma_start(s_b[:], b_s).then_inc(ld["bw"], 16)
            sp.dma_start(s_3[:], b_s3).then_inc(ld["bw"], 16)
            sp.dma_start(w_h1[:], b_h1).then_inc(ld["bh"], 16)
            sp.dma_start(w_h2[:], b_h2).then_inc(ld["bh"], 16)
            sp.dma_start(w_3[:], b_w3).then_inc(ld["bh"], 16)
            sp.dma_start(w_c[:], c_w).then_inc(ld["cw"], 16)
            sp.dma_start(w_o[:], c_wo).then_inc(ld["cw"], 16)
            sp.dma_start(b_o[:], c_bo).then_inc(ld["cw"], 16)
            sp.dma_start(sm[:], small).then_inc(ld["cw"], 16)
            sp.wait_ge(S["rk2"], CHUNKS)
            sp.wait_ge(S["o_a"], TILES)
            sp.dma_start(w_g[:], d_wg).then_inc(ld["dw"], 16)
            sp.dma_start(w_u[:], d_wu).then_inc(ld["dw"], 16)
            sp.dma_start(w_d[:], d_wd).then_inc(ld["dw"], 16)
            sp.dma_start(w_r[:], d_wr).then_inc(ld["dw"], 16)
            sp.dma_start(before[:].rearrange("p a b c -> p (a b c)"), before_in).then_inc(ld["dw"], 16)
            for c in range(CHUNKS):
                sp.wait_ge(S["xfin"], c + 1)
                sp.dma_start(out_dst[:, chunk(c), :], x[:, chunk(c), :]).then_inc(S["stored"], 16)
            sp.wait_ge(S["stored"], 16 * CHUNKS)

        @block.tensor
        def _(pe):
            mm = nc.tensor.matmul

            def turn_chunk(src, bank=turn):
                for k in range(CT):
                    last = nc.tensor.transpose(bank[:, k * P:(k + 1) * P], src[:, k, :], ident[:])
                return last

            pe.wait_ge(ld["idf"], 16)
            for c in range(CHUNKS):
                pe.wait_ge(S["xn_a"], c + 1)
                turn_chunk(xn).then_inc(S["tp_a"], 1)
                pe.wait_ge(S["xt_a"], c + 1)
                if c == 0:
                    pe.wait_ge(ld["aw"], 16)
                pe.wait_ge(S["rq2"], c)
                mm(ps[:, 0, :], w_a[:, 0, :], xt[:], start=True, stop=True)
                mm(ps[:, 1, :], w_a[:, 1, :], xt[:], start=True, stop=True).then_inc(S["qp_a"], 1)
                pe.wait_ge(S["rk2"], c)
                mm(ps[:, 2, :], w_a[:, 2, :], xt[:], start=True, stop=True)
                mm(ps[:, 3, :], w_a[:, 3, :], xt[:], start=True, stop=True).then_inc(S["kp_a"], 1)
                pe.wait_ge(S["vout"], c)
                for k in range(CT):
                    last = mm(ps[:, 4, k * P:(k + 1) * P], xt[:, k * P:(k + 1) * P], w_a[:, 4, :],
                              start=True, stop=True)
                last.then_inc(S["v_a"], 1)

            def width(i):
                return min(P * (i + 1) + 1, SEQ)

            def a_scores(t):
                b, i = divmod(t, BT)
                base = 2 * (t % 2)
                if t == 0:
                    pe.wait_ge(ld["con"], 32)
                    pe.wait_ge(S["rq2"], CHUNKS)
                    pe.wait_ge(S["rk2"], CHUNKS)
                pe.wait_ge(S["ropeq"], 2 * b + 2)
                pe.wait_ge(S["ropek"], 2 * b + 2)
                if t >= 2:
                    pe.wait_ge(S["e_a"], t - 1)
                w = width(i)
                for n0 in range(0, w, CHUNK):
                    n1 = min(w, n0 + CHUNK)
                    m0, m1 = max(n0, P * i), n1
                    bank = base + n0 // CHUNK
                    masked = m1 > m0
                    last = mm(ps[:, bank, 0:n1 - n0], q_t[:, b, i * P:(i + 1) * P], k_t[:, b, n0:n1],
                              start=True, stop=not masked)
                    if masked:
                        last = mm(ps[:, bank, m0 - n0:m1 - n0], ident_bf[:],
                                  mask[:, m0 - P * i:m1 - P * i], start=False, stop=True)
                last.then_inc(S["s_a"], 1)

            def a_turn(t):
                i = t % BT
                pe.wait_ge(S["e_a"], t + 1)
                if t == 0:
                    pe.wait_ge(S["vout"], CHUNKS)
                pe.wait_ge(S["pe_a"], t)
                for j in range(i + 1):
                    last = nc.tensor.transpose(ps[:, 4 + j // CT, (j % CT) * P:(j % CT + 1) * P],
                                               probs[:, t % 2, j * P:(j + 1) * P], ident[:])
                if i < BT - 1:
                    j = i + 1
                    last = nc.tensor.transpose(ps[0:1, 4 + j // CT, (j % CT) * P:(j % CT + 1) * P],
                                               probs[:, t % 2, j * P:j * P + 1], ident[:])
                last.then_inc(S["pt_a"], 1)

            def a_values(t):
                b, i = divmod(t, BT)
                pe.wait_ge(S["pe_a"], t + 1)
                if t >= 2:
                    pe.wait_ge(S["y_a"], t - 1)
                if t == 1:
                    pe.wait_ge(S["xt_a"], CHUNKS)
                o = ps[:, 6 + t % 2, 0:P]
                for j in range(i + 1):
                    last = mm(o, probs_t[:, t % 2, j * P:(j + 1) * P], v_a[:, b * BT + j, :],
                              start=(j == 0), stop=(i == BT - 1 and j == i))
                if i < BT - 1:
                    j = i + 1
                    last = mm(o, probs_t[0:1, t % 2, j * P:(j + 1) * P], v_a[0:1, b * BT + j, :],
                              start=False, stop=True)
                last.then_inc(S["o_a"], 1)

            for t in range(TILES + 2):
                if t < TILES:
                    a_scores(t)
                if 1 <= t <= TILES:
                    a_turn(t - 1)
                if t >= 2:
                    a_values(t - 2)

            def b_turn(c):
                pe.wait_ge(S["xn_b"], c + 1)
                if c == 0:
                    pe.wait_ge(S["xt_a"], CHUNKS)
                else:
                    pe.wait_ge(S["xt_b"], c)
                if c >= 3:
                    pe.wait_ge(S["xt_c"], c - 2)
                turn_chunk(xn).then_inc(S["tp_b"], 1)

            def c_prep(c):
                pe.wait_ge(S["xn_c"], c + 1)
                pe.wait_ge(S["xt_b"], min(c + 3, CHUNKS))
                turn_chunk(xn_c).then_inc(S["tp_c"], 1)
                pe.wait_ge(S["xt_c"], c + 1)
                if c == 0:
                    pe.wait_ge(ld["cw"], 64)
                for k in range(CT):
                    if CT * c + k >= 2:
                        pe.wait_ge(S["vraw_c"], CT * c + k - 1)
                    mm(ps[:, 5 + k % 2, 0:3 * P], xt_c[:, k * P:(k + 1) * P], w_c[:],
                       start=True, stop=True).then_inc(S["qkv_c"], 1)

            pe.wait_ge(S["y_a"], TILES)
            b_turn(0)
            pe.wait_ge(ld["bw"], 48)
            for c in range(CHUNKS):
                pe.wait_ge(S["xt_b"], c + 1)
                for m in range(KT_):
                    if m >= 2:
                        pe.wait_ge(S["h_b"], KT_ * c + m - 1)
                    elif c >= 1:
                        pe.wait_ge(S["g2_b"], KT_ * c)
                    for w in range(2):
                        last = mm(ps[:, 2 * (m % 2) + w, :], w_12[:, w, m * P:(m + 1) * P], xt[:],
                                  start=True, stop=True)
                    last.then_inc(S["gu_b"], 1)
                if c == 0:
                    pe.wait_ge(ld["bh"], 48)
                for o in range(KT_):
                    if o == 0:
                        pe.wait_ge(S["h_b"], KT_ * c + 3)
                    if o == 2:
                        pe.wait_ge(S["h_b"], KT_ * c + 4)
                    for k in range(KT_):
                        if o == 0 and k >= 2:
                            pe.wait_ge(S["h_b"], KT_ * c + k + 1)
                        last = mm(ps[:, o, :], w_h1[:, k, o * P:(o + 1) * P], hid[:, 0, k, :],
                                  start=(k == 0), stop=(k == KT_ - 1))
                    last.then_inc(S["m1_b"], 1)
                if c + 1 < CHUNKS:
                    b_turn(c + 1)
                if c >= 1:
                    c_prep(c - 1)
                for o in range(KT_):
                    pe.wait_ge(S["g1_b"], KT_ * c + o + 1)
                    for k in range(KT_):
                        if o == 0:
                            pe.wait_ge(S["g1_b"], KT_ * c + k + 1)
                        last = mm(ps[:, o, :], w_h2[:, k, o * P:(o + 1) * P], hid[:, 1, k, :],
                                  start=(k == 0), stop=(k == KT_ - 1))
                    last.then_inc(S["m2_b"], 1)
                pe.wait_ge(S["yo_b"], c)
                for k4 in range(CT):
                    for k in range(KT_):
                        if k4 == 0:
                            pe.wait_ge(S["g2_b"], KT_ * c + k + 1)
                        last = mm(ps[:, 4, k4 * P:(k4 + 1) * P], hid[:, 2, k, k4 * P:(k4 + 1) * P],
                                  w_3[:, k, :], start=(k == 0), stop=(k == KT_ - 1))
                last.then_inc(S["y_b"], 1)
            c_prep(CHUNKS - 1)

            def c_turn(which, n, u):
                src, ready = (u_q, "uq") if which == "q" else (u_k, "uk")
                pe.wait_ge(S[ready], n + 1)
                for j in range(BT):
                    last = nc.tensor.transpose(turn_bf[:, j * P:(j + 1) * P], src[:, u, j, :], ident_bf[:])
                last.then_inc(S["tq" if which == "q" else "tk"], 1)

            def c_scores(s, u, mt):
                keys = slice(mt * P, (mt + 1) * P)
                for base, k_op, free, done in ((0, k_s, "g", "dd"), (2, k_1, "z1", "l1"), (4, k_2, "z2", "l2")):
                    pe.wait_ge(S[free], s)
                    for half in range(2):
                        last = mm(ps[:, base + half, :], k_op[:, u, keys],
                                  q_s[:, u, half * CHUNK:(half + 1) * CHUNK], start=True, stop=True)
                    last.then_inc(S[done], 1)

            def c_values(s, u, mt):
                pe.wait_ge(S["e"], s + 1)
                for g4 in range(4):
                    last = mm(ps[VW * g4:VW * g4 + VW, 6, :], v_h[:, u, mt, :],
                              ee[:, mt % 2, g4 * CHUNK:(g4 + 1) * CHUNK],
                              start=(mt == 0), stop=(mt == BT - 1), skip_group_check=True)
                last.then_inc(S["av"], 1)

            def c_turn_out(n):
                pe.wait_ge(S["accout"], n + 1)
                for j in range(4):
                    last = nc.tensor.transpose(turn[:, j * P:(j + 1) * P], acc_sb[:, j * P:(j + 1) * P], ident[:])
                last.then_inc(S["to"], 1)

            def c_head(n, u, first, final, second=True):
                for mt in range(BT):
                    s = n * BT + mt
                    if mt < BT - 2:
                        c_scores(s + 2, u, mt + 2)
                    elif not final:
                        if mt == BT - 2:
                            pe.wait_ge(S["k12"], n + 2)
                            pe.wait_ge(S["qs"], n + 2)
                        c_scores(s + 2, 1 - u, mt + 2 - BT)
                    if mt == 0:
                        pe.wait_ge(S["vh"], n + 1)
                        if not first:
                            pe.wait_ge(S["accout"], n)
                    c_values(s, u, mt)
                    if mt == 0 and not final:
                        if second:
                            pe.wait_ge(S["oo"], n - 1)
                        c_turn("k", n + 1, 1 - u)
                    if mt == 2 and not final:
                        pe.wait_ge(S["ks"], n + 2)
                        c_turn("q", n + 1, 1 - u)
                    if mt == 4 and not first:
                        if not final:
                            pe.wait_ge(S["qs"], n + 2)
                        else:
                            pe.wait_ge(S["oo"], n - 1)
                        c_turn_out(n - 1)

            pe.wait_ge(S["xt_c"], CHUNKS)
            pe.wait_ge(S["vraw_c"], TILES)
            pe.wait_ge(S["yo_b"], CHUNKS)
            c_turn("k", 0, 0)
            pe.wait_ge(S["ks"], 1)
            c_turn("q", 0, 0)
            pe.wait_ge(S["qs"], 1)
            pe.wait_ge(S["k12"], 1)
            c_scores(0, 0, 0)
            c_scores(1, 0, 1)
            c_head(0, 0, True, False, False)
            c_head(1, 1, False, False, False)
            with pe.Fori(1, BATCH * HEADS // 2 - 1) as it:
                c_head(2 * it, 0, False, False)
                c_head(2 * it + 1, 1, False, False)
            c_head(BATCH * HEADS - 2, 0, False, False)
            c_head(BATCH * HEADS - 1, 1, False, True)
            pe.wait_ge(S["oo"], BATCH * HEADS - 1)
            c_turn_out(BATCH * HEADS - 1)

            def d_prep_out(c):
                pe.wait_ge(S["yc"], c + 1)
                pe.wait_ge(S["oo"], BATCH * HEADS)
                if c >= 1:
                    pe.wait_ge(S["xt_d"], c)
                turn_chunk(y_c).then_inc(S["ytp"], 1)
                pe.wait_ge(S["yt"], c + 1)
                if c == 0:
                    pe.wait_ge(S["const_c"], 1)
                if c >= 1:
                    pe.wait_ge(S["rcopy"], c)
                for k in range(CT):
                    last = mm(ps[:, 6, k * P:(k + 1) * P], y_ct[:, k * P:(k + 1) * P], w_os[:],
                              start=True, stop=True)
                last.then_inc(S["wo"], 1)

            def d_prep_in(c):
                pe.wait_ge(S["xn_d"], c + 1)
                turn_chunk(xn).then_inc(S["tp_d"], 1)

            def d_route(c):
                pe.wait_ge(S["xt_d"], c + 1)
                if c == 0:
                    pe.wait_ge(ld["dw"], 80)
                for k in range(CT):
                    last = mm(ps[:, 6, k * EXPERTS:(k + 1) * EXPERTS],
                              d_xt(c)[:, k * P:(k + 1) * P], w_r[:], start=True, stop=True)
                last.then_inc(S["rt_d"], 1)

            def d_up(c, e):
                n = EXPERTS * c + e
                if n >= 2:
                    pe.wait_ge(S["h_d"], n - 1)
                for w, wt in enumerate((w_g, w_u)):
                    last = mm(ps[:, 2 * (e % 2) + w, :], wt[:, e, :], d_xt(c), start=True, stop=True)
                last.then_inc(S["gu_d"], 1)

            def d_down(c, e):
                n = EXPERTS * c + e
                pe.wait_ge(S["h_d"], n + 1)
                if n >= 2:
                    pe.wait_ge(S["sc_d"], n - 1)
                for k in range(CT):
                    last = mm(ps[:, 4 + e % 2, k * P:(k + 1) * P], h_d[:, e % 2, k * P:(k + 1) * P],
                              w_d[:, e, :], start=True, stop=True)
                last.then_inc(S["eo_d"], 1)

            d_prep_out(0)
            d_prep_in(0)
            d_route(0)
            for c in range(CHUNKS):
                for e in range(EXPERTS):
                    d_up(c, e)
                    if e >= 1:
                        d_down(c, e - 1)
                    if e == 1 and c + 1 < CHUNKS:
                        d_prep_out(c + 1)
                    if e == 5 and c + 1 < CHUNKS:
                        d_prep_in(c + 1)
                d_down(c, EXPERTS - 1)
                if c + 1 < CHUNKS:
                    d_route(c + 1)

        @block.scalar
        def _(act):
            A = nc.scalar.activation
            me = Turn(act, s_self["act"])
            for c in range(CHUNKS):
                act.wait_ge(S["tp_a"], c + 1)
                act.wait_ge(S["v_a"], c)
                A(xt[:], turn, ACT.Copy).then_inc(S["xt_a"], 1)
                act.wait_ge(S["v_a"], c + 1)
                A(v_a[:, chunk(c), :].rearrange("p a b -> p (a b)"), ps[:, 4, :], ACT.Copy).then_inc(S["vout"], 1)
            banks = ps[:].rearrange("p a b -> p (a b)")

            def a_exp(t):
                i = t % BT
                w = min(P * (i + 1) + 1, SEQ)
                act.wait_ge(S["m_a"], t + 1)
                if t >= 2:
                    act.wait_ge(S["pt_a"], t - 1)
                base = 2 * CHUNK * (t % 2)
                A(probs[:, t % 2, 0:w], banks[:, base:base + w], ACT.Exp, bias=nmx[:, t:t + 1],
                  scale=ATT_SCALE, accum_out=rsum[:, t:t + 1]).then_inc(S["e_a"], 1)

            def a_turned(t):
                i = t % BT
                act.wait_ge(S["pt_a"], t + 1)
                if t >= 2:
                    act.wait_ge(S["o_a"], t - 1)
                w = P * (i + 1)
                src = banks[:, 4 * CHUNK:6 * CHUNK]
                last = A(probs_t[:, t % 2, 0:w], src[:, 0:w], ACT.Copy)
                if i < BT - 1:
                    last = A(probs_t[0:1, t % 2, w:w + P], src[0:1, w:w + P], ACT.Copy)
                last.then_inc(S["pe_a"], 1)

            for t in range(TILES + 1):
                if t < TILES:
                    a_exp(t)
                if t >= 1:
                    a_turned(t - 1)

            def b_xt(c):
                act.wait_ge(S["tp_b"], c + 1)
                act.wait_ge(S["gu_b"], KT_ * c) if c else act.wait_ge(S["v_a"], CHUNKS)
                A(xt[:], turn, ACT.Copy).then_inc(S["xt_b"], 1)

            def c_evac(c):
                act.wait_ge(S["tp_c"], c + 1)
                act.wait_ge(S["qkv_c"], CT * c)
                A(xt_c[:], turn, ACT.Copy).then_inc(S["xt_c"], 1)
                b, half = divmod(c, 2)
                for k in range(CT):
                    act.wait_ge(S["qkv_c"], CT * c + k + 1)
                    if k == 0:
                        act.wait_ge(S["qh_c"], c)
                    bank = ps[:, 5 + k % 2, :]
                    A(raw[:, :, :, k * VH:(k + 1) * VH],
                      bank[:, 0:2 * P].rearrange("p (a h v) -> p a h v", a=2, h=HEADS), ACT.Copy).then_inc(S["raw_c"], 1)
                    A(v_c[:, b * HEADS:(b + 1) * HEADS, half * CT + k, :],
                      bank[:, 2 * P:3 * P].rearrange("p (h v) -> p h v", h=HEADS), ACT.Copy).then_inc(S["vraw_c"], 1)

            def c_parts(c):
                b, half = divmod(c, 2)
                at = (slice(None), slice(None), slice(b * HEADS, (b + 1) * HEADS),
                      slice(half * CT * VH, (half + 1) * CT * VH))
                act.wait_ge(S["qh_c"], c + 1)
                A(part[0][at], sq[:], ACT.Copy).then_inc(S["hi_c"], 1)
                act.wait_ge(S["r1_c"], c + 1)
                A(part[1][at], raw2[:], ACT.Copy).then_inc(S["mid_c"], 1)

            raw2 = raw
            b_xt(0)
            for c in range(CHUNKS):
                if c == 0:
                    act.wait_ge(ld["bw"], 48)
                for m in range(KT_):
                    n = KT_ * c + m
                    act.wait_ge(S["gu_b"], n + 1)
                    if n >= 2:
                        act.wait_ge(S["h_b"], n - 1)
                    A(sg[:, m % 2, :], ps[:, 2 * (m % 2), :], ACT.Silu, scale=s_b[:, m:m + 1]).then_inc(S["sg_b"], 1)
                for o in range(KT_):
                    act.wait_ge(S["m1_b"], KT_ * c + o + 1)
                    if c:
                        act.wait_ge(S["m2_b"], KT_ * c)
                    A(hid[:, 1, o, :], ps[:, o, :], ACT.Gelu, scale=s_b[:, 8 + o:9 + o]).then_inc(S["g1_b"], 1)
                if c + 1 < CHUNKS:
                    b_xt(c + 1)
                if c >= 1:
                    c_evac(c - 1)
                for o in range(KT_):
                    act.wait_ge(S["m2_b"], KT_ * c + o + 1)
                    if c:
                        act.wait_ge(S["y_b"], c)
                    A(hid[:, 2, o, :], ps[:, o, :], ACT.Gelu, scale=s_b[:, 12 + o:13 + o]).then_inc(S["g2_b"], 1)
                if c == 0:
                    act.wait_ge(S["const_c"], 1)
                    me.step(A(tiny[:, 0:2], tiny[:, 0:2], ACT.Exp))
                    A(tiny[:, 8:17], tiny[:, 8:17], ACT.Tanh).then_inc(S["const_c"], 1)
                if c >= 1:
                    c_parts(c - 1)
            c_evac(CHUNKS - 1)
            c_parts(CHUNKS - 1)


            def tanh_step(s, u, mt):
                act.wait_ge(S["dd"], s + 1)
                act.wait_ge(S["z2"], s - 1)
                A(gg[:, mt % 2, :], banks[:, 0:2 * CHUNK], ACT.Tanh, scale=gain[:, u:u + 1]).then_inc(S["g"], 1)

            def head(n, u, final):
                for mt in range(BT):
                    s = n * BT + mt
                    if mt < BT - 1:
                        tanh_step(s + 1, u, mt + 1)
                    elif not final:
                        act.wait_ge(S["gcp"], n + 2)
                        tanh_step(s + 1, 1 - u, 0)
                    act.wait_ge(S["z2"], s + 1)
                    if final and mt == BT - 1:
                        act.wait_ge(S["av"], s - 1)
                    A(ee[:, mt % 2, :], zz[:, mt % 2, :], ACT.Exp).then_inc(S["e"], 1)

            act.wait_ge(S["gcp"], 1)
            act.wait_ge(S["dd"], 1)
            A(gg[:, 0, :], banks[:, 0:2 * CHUNK], ACT.Tanh, scale=gain[:, 0:1]).then_inc(S["g"], 1)
            head(0, 0, False)
            head(1, 1, False)
            with act.Fori(1, BATCH * HEADS // 2 - 1) as it:
                head(2 * it, 0, False)
                head(2 * it + 1, 1, False)
            head(BATCH * HEADS - 2, 0, False)
            head(BATCH * HEADS - 1, 1, True)

            def d_out(c):
                act.wait_ge(S["ytp"], c + 1)
                act.wait_ge(S["wo"], c)
                A(y_ct[:], turn, ACT.Copy).then_inc(S["yt"], 1)

            def d_in(c):
                act.wait_ge(S["tp_d"], c + 1)
                if c >= 2:
                    act.wait_ge(S["gu_d"], EXPERTS * (c - 1))
                A(d_xt(c), turn, ACT.Copy).then_inc(S["xt_d"], 1)

            def d_gate(c):
                act.wait_ge(S["rcopy"], c + 1)
                A(rt[:, 1], rt[:, 0], ACT.Tanh, scale=0.5).then_inc(S["tanh_d"], 1)
                act.wait_ge(S["dist_d"], c + 1)
                me.mark(A(rt[:, 3], rt[:, 2], ACT.Exp, scale=-1.0 / 0.1))
                A(rt[:, 4], rt[:, 2], ACT.Exp, scale=-1.0 / 0.3).then_inc(S["ex_d"], 1)

            d_out(0)
            d_in(0)
            d_gate(0)
            for c in range(CHUNKS):
                for e in range(EXPERTS):
                    n = EXPERTS * c + e
                    act.wait_ge(S["gu_d"], n + 1)
                    if n >= 2:
                        act.wait_ge(S["h_d"], n - 1)
                    A(sg_d[:, e % 2, :], ps[:, 2 * (e % 2), :], ACT.Silu).then_inc(S["sg_d"], 1)
                    if e == 1 and c + 1 < CHUNKS:
                        d_out(c + 1)
                    if e == 5 and c + 1 < CHUNKS:
                        d_in(c + 1)
                if c + 1 < CHUNKS:
                    d_gate(c + 1)

        @block.vector
        def _(dve):
            v = nc.vector
            me = Turn(dve, s_self["dve"])

            def rsqrt(dst, w):
                a, h, t = nv[:, 0:w], nh[:, 0:w], nt[:, 0:w]
                me.mark(v.tensor_scalar(h, a, -0.5, None, ALU.mult))
                me.step(v.tensor_scalar(dst.bitcast(I32), a.bitcast(I32), -0.5, RSQRT_MAGIC, ALU.mult, ALU.add))
                for _ in range(3):
                    me.step(v.tensor_tensor(t, dst, dst, ALU.mult))
                    me.step(v.tensor_tensor(t, t, h, ALU.mult))
                    me.step(v.scalar_tensor_tensor(dst, t, 1.5, dst, ALU.add, ALU.mult))

            def statistics(src):
                for k in range(CT):
                    me.mark(v.bn_stats(st[:, k, :], src[:, k, :]))
                me.wait()
                for k in range(CT):
                    me.mark(v.bn_aggr(mv[:, k, :], st[:, k, :]))
                me.wait()
                me.step(v.tensor_scalar(nv[:, 0:CT], mv[:, :, 1], LN_EPS, None, ALU.add))
                rsqrt(rstd[:, 0:CT], CT)

            def norm_in(src, dst, done):
                statistics(src)
                for k in range(CT):
                    last = v.tensor_scalar(dst[:, k, :], src[:, k, :], mv[:, k, 0:1], rstd[:, k:k + 1],
                                           ALU.subtract, ALU.mult)
                    if k < CT - 1:
                        me.mark(last)
                last.then_inc(S[done], 1)

            def norm_out(src, c, done=None):
                statistics(src)
                for k in range(CT):
                    me.mark(v.tensor_scalar(src[:, k, :], src[:, k, :], mv[:, k, 0:1], rstd[:, k:k + 1],
                                            ALU.subtract, ALU.mult))
                me.wait()
                last = v.tensor_tensor(x[:, chunk(c), :], x[:, chunk(c), :], src, ALU.add)
                if done:
                    last.then_inc(S[done], 1)
                else:
                    me.step(last)

            for c in range(CHUNKS):
                dve.wait_ge(ld[f"x{c}"], 16)
                dve.wait_ge(S["tp_a"], c)
                norm_in(x[:, chunk(c), :], xn, "xn_a")
                if c == 0:
                    dve.wait_ge(ld["tab"], 16)
                b, half = divmod(c, 2)
                at = slice(half * CHUNK, (half + 1) * CHUNK)
                for i, (dst, bank, got, r1, r2, summed) in enumerate(
                        ((q_t, 0, "qp_a", "rq1", "rq2", "ropeq"), (k_t, 2, "kp_a", "rk1", "rk2", "ropek"))):
                    dve.wait_ge(S[got], c + 1)
                    v.tensor_tensor(dst[:, b, at], ps[:, bank, :], tab[:, 0, at], ALU.mult).then_inc(S[r1], 1)
                    dve.wait_ge(S[summed], c)
                    v.tensor_tensor(rot[:, i, :], ps[:, bank + 1, :], tab[:, 1, at], ALU.mult).then_inc(S[r2], 1)

            banks = ps[:].rearrange("p a b -> p (a b)")

            def a_max(t):
                i = t % BT
                w = min(P * (i + 1) + 1, SEQ)
                dve.wait_ge(S["s_a"], t + 1)
                base = 2 * CHUNK * (t % 2)
                me.step(v.tensor_reduce(mx[:, t:t + 1], banks[:, base:base + w], AX.X, ALU.max))
                v.tensor_scalar(nmx[:, t:t + 1], mx[:, t:t + 1], -ATT_SCALE, None, ALU.mult).then_inc(S["m_a"], 1)

            def a_post(t):
                dve.wait_ge(S["e_a"], t + 1)
                me.step(v.reciprocal(rinv[:, t:t + 1], rsum[:, t:t + 1]))
                dve.wait_ge(S["o_a"], t + 1)
                v.tensor_scalar(y_a[:, t, :], ps[:, 6 + t % 2, 0:P], rinv[:, t:t + 1],
                                None, ALU.mult).then_inc(S["y_a"], 1)
                if t % CT == CT - 1:
                    c = t // CT
                    dve.wait_ge(S["y_a"], t + 1)
                    norm_out(y_a[:, chunk(c), :], c)

            for t in range(TILES + 2):
                if t < TILES:
                    a_max(t)
                if t >= 2:
                    a_post(t - 2)

            def b_hidden(c, m):
                n = KT_ * c + m
                if c:
                    dve.wait_ge(S["m1_b"], KT_ * c)
                if n == 0:
                    dve.wait_ge(ld["bw"], 48)
                dve.wait_ge(S["sg_b"], n + 1)
                v.scalar_tensor_tensor(hid[:, 0, m, :], ps[:, 2 * (m % 2) + 1, :], s_b[:, 4 + m:5 + m],
                                       sg[:, m % 2, :], ALU.mult, ALU.mult).then_inc(S["h_b"], 1)

            def b_out(c):
                dve.wait_ge(S["y_b"], c + 1)
                v.tensor_tensor(y[:], ps[:, 4, :].rearrange("p (a b) -> p a b", a=CT),
                                s_3[:].unsqueeze(1).to_broadcast([P, CT, P]), ALU.mult).then_inc(S["yo_b"], 1)
                dve.wait_ge(S["yo_b"], c + 1)
                norm_out(y[:], c)

            def c_const():
                dve.wait_ge(ld["cw"], 64)
                me.step(v.tensor_tensor(tiny[:, 32:48].rearrange("p (a b) -> p a b", a=2),
                                        sm[:, 0:32].rearrange("p (a c b) -> p a c b", a=2, c=2)[:, :, 0, :],
                                        sm[:, 0:32].rearrange("p (a c b) -> p a c b", a=2, c=2)[:, :, 1, :], ALU.mult))
                me.mark(v.tensor_reduce(tiny[:, 0:2], tiny[:, 32:48].rearrange("p (a b) -> p a b", a=2), AX.X, ALU.add))
                me.step(v.tensor_reduce(tiny[:, 48:49], sm[:, SM_DELTA:SM_DELTA + HEADS], AX.X, ALU.add))
                me.step(v.tensor_scalar(tiny[:, 48:49], tiny[:, 48:49], 1.0 / HEADS, None, ALU.mult))
                me.mark(v.tensor_scalar(tiny[:, 8:16], sm[:, SM_DELTA:SM_DELTA + HEADS], tiny[:, 48:49], None, ALU.subtract))
                v.tensor_scalar(tiny[:, 16:17], sm[:, SM_RAW:SM_RAW + 1], 0.5, None, ALU.mult)
                me.step(v.tensor_scalar(w_os[:], w_o[:], sm[:, SM_SUBLN:SM_SUBLN + 1], 1.0 - LAMBDA_INIT, ALU.mult, ALU.mult))

            for c in [0]:
                dve.wait_ge(S["tp_a"], CHUNKS)
            norm_in(x[:, chunk(0), :], xn, "xn_b")
            raise_ = None
            c_consts_done = False

            def c_in(c):
                dve.wait_ge(S["tp_c"], c)
                norm_in(x[:, chunk(c), :], xn_c, "xn_c")

            def c_norms(c):
                b, half = divmod(c, 2)
                at = (slice(None), slice(None), slice(b * HEADS, (b + 1) * HEADS),
                      slice(half * CT * VH, (half + 1) * CT * VH))
                dve.wait_ge(S["sq_c"], c + 1)
                me.step(v.tensor_reduce(ss[:], sq[:].rearrange("p a h (g d) -> p (a h g) d", d=DH), AX.X, ALU.add))
                me.step(v.tensor_scalar(nv[:], ss[:], 1e-12, 1e38, ALU.max, ALU.min))
                rsqrt(rstd[:], P)
                me.step(v.tensor_tensor(rstd[:], rstd[:], cs_tab[:].rearrange("p a h k c -> p (a h k c)"), ALU.mult))
                v.tensor_tensor(sq[:].rearrange("p a h (g d) -> p (a h g) d", d=DH),
                                raw[:].rearrange("p a h (g d) -> p (a h g) d", d=DH),
                                rstd[:].unsqueeze(2).to_broadcast([P, P, DH]), ALU.mult).then_inc(S["qh_c"], 1)
                dve.wait_ge(S["hi_c"], c + 1)
                v.tensor_tensor(raw[:], sq[:], part[0][at], ALU.subtract).then_inc(S["r1_c"], 1)
                dve.wait_ge(S["mid_c"], c + 1)
                v.tensor_tensor(part[2][at], raw[:], part[1][at], ALU.subtract).then_inc(S["lo_c"], 1)

            for c in range(CHUNKS):
                for m in range(KT_):
                    if m == 2 and c:
                        b_out(c - 1)
                    b_hidden(c, m)
                if c + 1 < CHUNKS:
                    dve.wait_ge(S["tp_b"], c + 1)
                    norm_in(x[:, chunk(c + 1), :], xn, "xn_b")
                if c == 0:
                    c_const()
                    v.tensor_scalar(tiny[:, 50:51], tiny[:, 48:49], 1.0, None, ALU.mult).then_inc(S["const_c"], 1)
                if c >= 1:
                    c_in(c - 1)
                    if c == 1:
                        c_table(dve, v, me)
                    c_norms(c - 1)
            b_out(CHUNKS - 1)
            c_in(CHUNKS - 1)
            c_norms(CHUNKS - 1)

            def z_step(s, mt):
                dve.wait_ge(S["g"], s + 1)
                dve.wait_ge(S["l1"], s + 1)
                v.tensor_tensor(zz[:, mt % 2, 0:SEQ], banks[:, 2 * CHUNK:4 * CHUNK], gg[:, mt % 2, :],
                                ALU.add).then_inc(S["z1"], 1)
                dve.wait_ge(S["l2"], s + 1)
                v.scalar_tensor_tensor(zz[:, mt % 2, SEQ:2 * SEQ], banks[:, 4 * CHUNK:6 * CHUNK], -1.0,
                                       gg[:, mt % 2, :], ALU.mult, ALU.subtract).then_inc(S["z2"], 1)

            def q_evac(n, u):
                dve.wait_ge(S["tq"], n + 1)
                v.tensor_copy(q_s[:, u, :], turn_bf).then_inc(S["qs"], 1)

            def k_evac(n, u):
                dve.wait_ge(S["tk"], n + 1)
                v.tensor_copy(k_s[:, u, :], turn_bf).then_inc(S["ks"], 1)

            def k_halves(n, u):
                dve.wait_ge(S["ks"], n + 1)
                v.tensor_scalar(k_1[:, u, :], k_s[:, u, :], sm[:, SM_HALF:SM_HALF + 1], None, ALU.mult)
                v.tensor_scalar(k_2[:, u, :], k_s[:, u, :], sm[:, SM_HALF + 1:SM_HALF + 2], None,
                                ALU.mult).then_inc(S["k12"], 1)

            def acc_out(n):
                dve.wait_ge(S["av"], BT * (n + 1))
                dve.wait_ge(S["to"], n)
                v.tensor_copy(acc_sb[:], ps[:, 6, :]).then_inc(S["accout"], 1)

            def o_evac(n):
                dve.wait_ge(S["to"], n + 1)
                v.tensor_copy(o_all[:, n, :, :, :].rearrange("p c g v -> p (c g) v") if isinstance(n, int) else
                              o_flat[:, n, :, :],
                              turn.rearrange("p (c w) -> p c w", w=VW)[:, :, 0:VH + 1]).then_inc(S["oo"], 1)

            o_flat = o_all[:].rearrange("p n c g v -> p n (c g) v")

            def head(n, u, first, final):
                for mt in range(BT):
                    z_step(n * BT + mt, mt)
                    if mt == 1 and not first:
                        acc_out(n - 1)
                    if mt == 2 and not final:
                        k_evac(n + 1, 1 - u)
                    if mt == 3 and not final:
                        k_halves(n + 1, 1 - u)
                    if mt == 4 and not final:
                        q_evac(n + 1, 1 - u)
                    if mt == 6 and not first:
                        o_evac(n - 1)

            k_evac(0, 0)
            k_halves(0, 0)
            q_evac(0, 0)
            head(0, 0, True, False)
            head(1, 1, False, False)
            with dve.Fori(1, BATCH * HEADS // 2 - 1) as it:
                head(2 * it, 0, False, False)
                head(2 * it + 1, 1, False, False)
            head(BATCH * HEADS - 2, 0, False, False)
            head(BATCH * HEADS - 1, 1, False, True)
            acc_out(BATCH * HEADS - 1)
            o_evac(BATCH * HEADS - 1)

            def heads_out(c):
                b, half = divmod(c, 2)
                o = o_all[:, b * HEADS:(b + 1) * HEADS, :, :, :].rearrange("p h c g v -> p (h c) g v")
                dve.wait_ge(S["oo"], BATCH * HEADS)
                for comp in range(2):
                    me.mark(v.reciprocal(r_o[:, comp, :], o[:, :, 2 * comp + half, VH]))
                me.wait()
                me.step(v.tensor_scalar(r_o[:, 1, :], r_o[:, 1, :], nlam[:, 0:1], None, ALU.mult))
                for comp in range(2):
                    me.mark(v.tensor_tensor(t_o[:, comp], o[:, :, 2 * comp + half, 0:VH],
                                            r_o[:, comp, :].unsqueeze(2).to_broadcast([P, HEADS * CT, VH]), ALU.mult))
                me.wait()
                me.step(v.tensor_tensor(t_o[:, 0], t_o[:, 0], t_o[:, 1], ALU.add))
                me.step(v.tensor_tensor(t_o[:, 1], t_o[:, 0], t_o[:, 0], ALU.mult))
                me.step(v.tensor_reduce(ss[:, 0:HEADS * CT], t_o[:, 1], AX.X, ALU.add))
                me.step(v.tensor_scalar(nv[:, 0:HEADS * CT], ss[:, 0:HEADS * CT], 1.0 / VH, RMS_EPS, ALU.mult, ALU.add))
                rsqrt(rstd[:, 0:HEADS * CT], HEADS * CT)
                dve.wait_ge(S["ytp"], c)
                v.tensor_tensor(y_c[:].rearrange("p c (h v) -> p h c v", h=HEADS),
                                t_o[:, 0].rearrange("p (h c) v -> p h c v", h=HEADS),
                                rstd[:, 0:HEADS * CT].rearrange("p (h c) -> p h c", h=HEADS).unsqueeze(3)
                                .to_broadcast([P, HEADS, CT, VH]), ALU.mult).then_inc(S["yc"], 1)

            def wo_out(c):
                dve.wait_ge(S["wo"], c + 1)
                me.step(v.tensor_tensor(y[:], ps[:, 6, :].rearrange("p (a b) -> p a b", a=CT),
                                        b_o[:].unsqueeze(1).to_broadcast([P, CT, P]), ALU.add))
                norm_out(y[:], c)

            def d_in(c):
                if c == 0:
                    dve.wait_ge(S["tp_b"], CHUNKS)
                dve.wait_ge(S["tp_d"], c)
                norm_in(x[:, chunk(c), :], xn, "xn_d")

            def route_a(c):
                dve.wait_ge(S["rt_d"], c + 1)
                if c == 0:
                    me.step(v.reciprocal(rs1[:, 3, 0:1], sm[:, SM_TEMP:SM_TEMP + 1]))
                v.tensor_scalar(rt[:, 0].rearrange("p a b -> p (a b)"), ps[:, 6, 0:CT * EXPERTS],
                                rs1[:, 3, 0:1], None, ALU.mult).then_inc(S["rcopy"], 1)
                dve.wait_ge(S["tanh_d"], c + 1)
                me.step(v.tensor_scalar(rt[:, 1], rt[:, 1], 0.5, 0.5, ALU.mult, ALU.add))
                me.step(v.tensor_scalar(rt[:, 5], rt[:, 1], -GOLDEN, None, ALU.add))
                me.mark(v.tensor_scalar(rt[:, 6], rt[:, 1], ZONE_LOW, None, ALU.is_ge))
                me.mark(v.tensor_scalar(rt[:, 7], rt[:, 1], ZONE_HIGH, None, ALU.is_le))
                v.scalar_tensor_tensor(rt[:, 2], rt[:, 5], -1.0, rt[:, 5], ALU.mult, ALU.max).then_inc(S["dist_d"], 1)
                me.wait()
                me.step(v.tensor_tensor(rt[:, 6], rt[:, 6], rt[:, 7], ALU.mult))

            def route_b(c):
                w = wts[:, c % 2]
                wide = [P, CT, EXPERTS]
                four = [P, CT, EXPERTS, EXPERTS]
                dve.wait_ge(S["ex_d"], c + 1)
                if c == 0:
                    dve.wait_ge(ld["dw"], 80)
                me.mark(v.tensor_tensor(rt[:, 3], rt[:, 3], rt[:, 6], ALU.mult))
                mine = rt[:, 4].unsqueeze(3).to_broadcast(four)
                others = rt[:, 4].unsqueeze(2).to_broadcast(four)
                for k in range(CT):
                    me.mark(v.tensor_tensor(pair[:, 0, k], rt[:, 4, k].unsqueeze(1).to_broadcast([P, EXPERTS, EXPERTS]),
                                            rt[:, 4, k].unsqueeze(2).to_broadcast([P, EXPERTS, EXPERTS]), ALU.is_gt))
                    me.mark(v.tensor_tensor(pair[:, 1, k], rt[:, 4, k].unsqueeze(1).to_broadcast([P, EXPERTS, EXPERTS]),
                                            rt[:, 4, k].unsqueeze(2).to_broadcast([P, EXPERTS, EXPERTS]), ALU.is_equal))
                me.wait()
                me.step(v.tensor_tensor(pair[:, 1], pair[:, 1], before[:], ALU.mult))
                me.step(v.tensor_tensor(pair[:, 0], pair[:, 0], pair[:, 1], ALU.add))
                me.mark(v.tensor_reduce(rt[:, 5], pair[:, 0], AX.X, ALU.add))
                me.mark(v.tensor_reduce(rs1[:, 0], rt[:, 3], AX.X, ALU.add))
                me.wait()
                me.mark(v.scalar_tensor_tensor(rt[:, 7], rt[:, 5], 1.5, rt[:, 4], ALU.is_lt, ALU.mult))
                me.step(v.tensor_scalar(rs1[:, 1], rs1[:, 0], 1e-8, None, ALU.is_lt))
                me.step(v.tensor_reduce(rs1[:, 0], rt[:, 7], AX.X, ALU.add))
                me.step(v.tensor_scalar(rs1[:, 0], rs1[:, 0], 1e-8, None, ALU.max))
                me.step(v.reciprocal(rs1[:, 2], rs1[:, 0]))
                me.mark(v.tensor_tensor(rs1[:, 2], rs1[:, 2], rs1[:, 1], ALU.mult))
                me.step(v.tensor_scalar(rs1[:, 1], rs1[:, 1], -1.0, 1.0, ALU.mult, ALU.add))
                me.mark(v.tensor_tensor(rt[:, 3], rt[:, 3], rs1[:, 1].unsqueeze(2).to_broadcast(wide), ALU.mult))
                me.step(v.tensor_tensor(rt[:, 7], rt[:, 7], rs1[:, 2].unsqueeze(2).to_broadcast(wide), ALU.mult))
                me.step(v.tensor_tensor(rt[:, 3], rt[:, 3], rt[:, 7], ALU.add))
                me.step(v.tensor_reduce(rs1[:, 0], rt[:, 3], AX.X, ALU.add))
                me.step(v.tensor_scalar(rs1[:, 0], rs1[:, 0], 1e-8, None, ALU.max))
                me.step(v.reciprocal(rs1[:, 2], rs1[:, 0]))
                me.step(v.tensor_tensor(w, rt[:, 3], rs1[:, 2].unsqueeze(2).to_broadcast(wide), ALU.mult))

            def d_hidden(c, e):
                n = EXPERTS * c + e
                dve.wait_ge(S["sg_d"], n + 1)
                if n >= 2:
                    dve.wait_ge(S["eo_d"], n - 1)
                v.tensor_tensor(h_d[:, e % 2, :], ps[:, 2 * (e % 2) + 1, :], sg_d[:, e % 2, :],
                                ALU.mult).then_inc(S["h_d"], 1)

            def d_scale(c, e):
                n = EXPERTS * c + e
                dve.wait_ge(S["eo_d"], n + 1)
                if n >= 2:
                    dve.wait_ge(S["ad_d"], n - 1)
                v.tensor_tensor(e_out[:, e % 2], ps[:, 4 + e % 2, :].rearrange("p (a b) -> p a b", a=CT),
                                wts[:, c % 2, :, e].unsqueeze(2).to_broadcast([P, CT, P]),
                                ALU.mult).then_inc(S["sc_d"], 1)

            heads_out(0)
            wo_out(0)
            d_in(0)
            route_a(0)
            route_b(0)
            heads_out(1)
            for c in range(CHUNKS):
                for e in range(EXPERTS):
                    d_hidden(c, e)
                    if e >= 1:
                        d_scale(c, e - 1)
                    if e == 2 and c + 1 < CHUNKS:
                        wo_out(c + 1)
                    if e == 3 and c + 1 < CHUNKS:
                        d_in(c + 1)
                    if e == 5 and c + 2 < CHUNKS:
                        heads_out(c + 2)
                d_scale(c, EXPERTS - 1)
                if c + 1 < CHUNKS:
                    route_a(c + 1)
                    route_b(c + 1)
                dve.wait_ge(S["ad_d"], EXPERTS * (c + 1))
                norm_out(y_d(c), c, "xfin")

        @block.gpsimd
        def _(pool):
            g = nc.gpsimd
            me = Turn(pool, s_self["pool"])

            for t in (u_q, u_k):
                me.step(g.memset(t[:].rearrange("p a b c -> p (a b c)"), 0.0))
            me.step(g.memset(v_h[:].rearrange("p a b c -> p (a b c)"), 0.0))
            me.step(g.memset(v_h[:, :, :, VH:VH + 1].rearrange("p a b c -> p (a b) c"), 1.0))
            for c in range(CHUNKS):
                b, half = divmod(c, 2)
                at = slice(half * CHUNK, (half + 1) * CHUNK)
                for i, (dst, r1, r2, summed) in enumerate(((q_t, "rq1", "rq2", "ropeq"), (k_t, "rk1", "rk2", "ropek"))):
                    pool.wait_ge(S[r1], c + 1)
                    pool.wait_ge(S[r2], c + 1)
                    g.tensor_tensor(dst[:, b, at], dst[:, b, at], rot[:, i, :], ALU.add).then_inc(S[summed], 1)
            for c in range(CHUNKS):
                pool.wait_ge(S["raw_c"], CT * (c + 1))
                pool.wait_ge(S["hi_c"], c)
                pool.wait_ge(S["r1_c"], c)
                g.tensor_tensor(sq[:], raw[:], raw[:], ALU.mult).then_inc(S["sq_c"], 1)

            q_parts = (0, 0, 1, 0, 2, 1)
            k_parts = (0, 1, 0, 2, 0, 1)

            def spread(dst, which, parts, n, u, done):
                for seg, i in enumerate(parts):
                    out_ap = dst[:, u].rearrange("p t (c r) -> p t c r", c=2)[:, :, :, seg * DH:(seg + 1) * DH]
                    in_ap = part[i][:, which, n, :].rearrange("p (t c d) -> p t c d", t=BT, c=2)
                    last = g.tensor_scalar(out_ap, in_ap, 1.0, None, ALU.mult)
                last.then_inc(S[done], 1)

            def build(n, u):
                if n >= 2:
                    pool.wait_ge(S["tk"], n - 1)
                spread(u_k, 1, k_parts, n, u, "uk")
                if n >= 2:
                    pool.wait_ge(S["tq"], n - 1)
                spread(u_q, 0, q_parts, n, u, "uq")
                if n >= 2:
                    pool.wait_ge(S["g"], BT * (n - 1))
                g.tensor_scalar(gain[:, u:u + 1], gains[:, n:n + 1], 1.0, None, ALU.mult).then_inc(S["gcp"], 1)
                if n >= 2:
                    pool.wait_ge(S["av"], BT * (n - 1))
                g.tensor_scalar(v_h[:, u, :, 0:VH], v_c[:, n, :, :], 1.0, None, ALU.mult).then_inc(S["vh"], 1)

            pool.wait_ge(S["lo_c"], CHUNKS)
            pool.wait_ge(S["vraw_c"], TILES)
            pool.wait_ge(ld["cw"], 64)
            for b in range(BATCH):
                last = g.tensor_scalar(gains[:, b * HEADS:(b + 1) * HEADS], sm[:, SM_GAIN:SM_GAIN + HEADS], 1.0, None, ALU.mult)
                me.step(last)
            for n in range(BATCH * HEADS):
                build(n, n % 2)

            for c in range(CHUNKS):
                for e in range(EXPERTS):
                    n = EXPERTS * c + e
                    pool.wait_ge(S["sc_d"], n + 1)
                    if e == 0:
                        if c >= 2:
                            pool.wait_ge(S["xfin"], c - 1)
                        g.tensor_scalar(y_d(c), e_out[:, 0], 1.0, None, ALU.mult).then_inc(S["ad_d"], 1)
                    else:
                        pool.wait_ge(S["ad_d"], n)
                        g.tensor_tensor(y_d(c), y_d(c), e_out[:, e % 2], ALU.add).then_inc(S["ad_d"], 1)

        
_OUTS = (BATCH, SEQ, P)


def kernel(**inputs):
    import ml_dtypes
    import numpy as _np
    import concourse.bacc as _bacc
    from concourse import mybir as _mybir
    from concourse.bass_utils import run_bass_kernel_spmd as _run

    f = {k: _np.asarray(v) for k, v in inputs.items()}

    order = _np.concatenate([_np.arange(0, P, 2), _np.arange(1, P, 2)])
    swapped = _np.concatenate([order[P // 2:], order[:P // 2]])
    wq, wk, wv = f["L0_attn_Wq"], f["L0_attn_Wk"], f["L0_attn_Wv"]
    a_w = _np.concatenate([wq[order].T, wq[swapped].T, wk[order].T, wk[swapped].T, wv.T], axis=1)
    b_w12 = _np.concatenate([f["L0_ffn_w1_w"].T, f["L0_ffn_w2_w"].T], axis=1)

    def by_k(w):
        return w.T.reshape(-1, P, w.shape[0]).transpose(1, 0, 2)

    def cols(s):
        return s.reshape(-1, P).T

    def rows(s):
        return _np.broadcast_to(s.reshape(1, -1), (P, s.size))

    b_s = _np.concatenate([cols(f[f"L0_ffn_{n}_s"]) for n in ("w1", "w2", "h1", "h2")], axis=1)
    c_w = _np.concatenate([f["L1_attn_Wq"].T, f["L1_attn_Wk"].T, f["L1_attn_Wv"].T], axis=1)
    small = _np.concatenate([rows(f["L1_attn_" + n]) for n in (
        "lambda_q1", "lambda_k1", "lambda_q2", "lambda_k2", "delta_gain", "cos_head_delta",
        "cos_logit_scale_raw")] + [rows(f["L1_ffn_temperature"]), _np.tile(f["L1_attn_subln_weight"], HEADS)[:, None],
        (_np.arange(P)[:, None] // (P // 2) == _np.arange(2)[None, :]).astype(_np.float32)], axis=1)

    theta = (_np.float32(10000.0) ** (_np.float32(-2.0) * _np.arange(P // 2, dtype=_np.float32) / _np.float32(P))).astype(_np.float32)
    ang = (_np.arange(SEQ, dtype=_np.float32)[:, None] * theta[None, :]).astype(_np.float32).T
    cos, sin = _np.cos(ang), _np.sin(ang)
    rope = _np.stack([_np.concatenate([cos, cos]), _np.concatenate([-sin, sin])], axis=1).astype(_np.float32)
    eye = _np.eye(P, dtype=_np.float32)
    mask = _np.where(_np.arange(P + 1)[None, :] <= _np.arange(P)[:, None] + 1, 0.0, MASKED).astype(ml_dtypes.bfloat16)
    before = (_np.arange(EXPERTS)[None, :] < _np.arange(EXPERTS)[:, None]).astype(_np.float32)
    before = _np.broadcast_to(before.reshape(1, 1, -1), (P, CT, EXPERTS * EXPERTS)).reshape(P, -1)

    arrays = {
        "x": f["L0_attn_x"], "a_w": a_w, "rope": rope, "b_w12": b_w12, "b_h1": by_k(f["L0_ffn_h1_w"]),
        "b_h2": by_k(f["L0_ffn_h2_w"]), "b_w3": by_k(f["L0_ffn_w3_w"]), "b_s": b_s,
        "b_s3": rows(f["L0_ffn_w3_s"]), "c_w": c_w, "c_wo": f["L1_attn_Wo"].T, "c_bo": rows(f["L1_attn_bo"]),
        "small": small, "d_wg": f["L1_ffn_Wg"].transpose(1, 0, 2), "d_wu": f["L1_ffn_Wu"].transpose(1, 0, 2),
        "d_wd": f["L1_ffn_Wd"].transpose(1, 0, 2), "d_wr": f["L1_ffn_Wr"], "ident": eye,
        "ident_bf": eye.astype(ml_dtypes.bfloat16), "mask": mask, "before": before,
    }
    nc = _bacc.Bacc("TRN2", target_bir_lowering=False, num_devices=1)
    feed, args = {}, []
    for name, a in arrays.items():
        a = _np.ascontiguousarray(a)
        feed[f"in_{name}"] = a
        args.append(nc.dram_tensor(f"in_{name}", a.shape, _mybir.dt.from_np(a.dtype), kind="ExternalInput").ap())
    args.append(nc.dram_tensor("out_0", _OUTS, F32, kind="ExternalOutput").ap())
    sandwich(nc, *args)
    r = _run(nc, [feed], core_ids=[0])
    return r.results[0]["out_0"]
```

```python
from contextlib import ExitStack

import numpy as np

import concourse.bass as bass
from concourse import mybir

F32 = mybir.dt.float32
BF16 = mybir.dt.bfloat16
I32 = mybir.dt.int32
ALU = mybir.AluOpType
ACT = mybir.ActivationFunctionType
AX = mybir.AxisListType

P = 128
BATCH, SEQ = 2, 1024
TILES = BATCH * SEQ // P
BT = SEQ // P
CT = 4
CHUNK = CT * P
CHUNKS = TILES // CT
HID = 512
KT_ = HID // P
HEADS, DH = 8, 8
VH = 2 * DH
VW = 32
PARTS = 6
EXPERTS = 8
LN_EPS = 1e-5
RMS_EPS = 1e-5
ATT_SCALE = float(P) ** -0.5
MASKED = -1e30
RSQRT_MAGIC = float(0x5F3759DF)
GOLDEN = float(1.0 / np.e)
ZONE_LOW = float(np.float32(0.5 - np.log(4.0 / 3.0)))
ZONE_HIGH = 0.5
COS_MAX = 15.0
LAMBDA_INIT = 0.5

SM_LAM, SM_GAIN, SM_DELTA, SM_RAW, SM_TEMP, SM_SUBLN, SM_HALF = 0, 32, 40, 48, 49, 50, 51
SM_W = 53
NORMS = [("a_in", c) for c in range(4)] + [("a_out", 0), ("b_in", 0), ("a_out", 1), ("a_out", 2), ("a_out", 3),
         ("b_in", 1), ("b_out", 0), ("b_in", 2), ("c_in", 0), ("b_out", 1), ("b_in", 3), ("c_in", 1),
         ("b_out", 2), ("c_in", 2), ("b_out", 3), ("c_in", 3), ("c_out", 0), ("d_in", 0), ("c_out", 1),
         ("d_in", 1), ("c_out", 2), ("d_out", 0), ("d_in", 2), ("c_out", 3), ("d_in", 3), ("d_out", 1),
         ("d_out", 2), ("d_out", 3)]
BANK_TURN = 7


NH = BATCH * HEADS


def turning(n, mt):
    last = n == NH - 1
    if mt == 0:
        return ("x", 1) if last else ("k", n + 1)
    if mt == 2:
        return ("route", 0) if last else ("q", n + 1)
    if mt == 4:
        return ("o", n - 1) if n else ("late turn", 0)
    if mt == 6:
        if n < CT:
            return ("late qkv", n)
        return {10: ("y", 0), 11: ("wo", 0), 12: ("y", 1), 13: ("wo", 1), 14: ("x", 0), 15: ("route", 1)}.get(n)
    return None


TURNS = [("k", 0), ("q", 0)] + [u for n in range(NH) for mt in range(BT) if (u := turning(n, mt))] + [("o", NH - 1)]


def turns_done(use):
    return TURNS.index(use) + 1


class Turn:

    def __init__(self, eng, sem, start=0):
        self.eng, self.sem, self.n = eng, sem, start

    def mark(self, ins):
        self.n += 1
        ins.then_inc(self.sem, 1)

    def wait(self):
        self.eng.wait_ge(self.sem, self.n)

    def step(self, ins):
        self.mark(ins)
        self.wait()


def sandwich(nc, x_in, a_w, rope, b_w12, b_h1, b_h2, b_w3, b_s, b_s3, c_w, c_wo, c_bo, small,
             d_wg, d_wu, d_wd, d_wr, ident_in, ident_bf_in, mask_in, before_in, out):
    with ExitStack() as ctx:
        def sb(name, shape, dt=F32):
            return ctx.enter_context(nc.sbuf_tensor(name, shape, dt))

        def sem(name):
            return ctx.enter_context(nc.semaphore(name))

        x = sb("x_res", [P, TILES, P])
        xn = sb("xn", [P, CT, P])
        xn_c = sb("xn_c", [P, CT, P])
        xn_2 = (xn, xn_c)
        xt = sb("xt", [P, CHUNK])
        xt_c = sb("xt_c", [P, CHUNK])
        y = sb("y", [P, CT, P])
        ident = sb("ident", [P, P])
        ident_bf = sb("ident_bf", [P, P], BF16)
        mask = sb("mask", [P, P + 1], BF16)
        before = sb("before", [P, EXPERTS, EXPERTS])
        st = sb("st", [P, 2, CT, 6])
        mv = sb("mv", [P, len(NORMS), CT, 2])
        rs = sb("rs", [P, len(NORMS), CT])
        half_down = sb("half_down", [P, CT])
        nv = sb("nv", [P, P])
        nh = sb("nh", [P, P])
        nt = sb("nt", [P, P])
        rstd = sb("rstd", [P, P])
        w_a = sb("w_a", [P, 5, P])
        tab = sb("tab", [P, 2, SEQ])
        qkv_a = sb("qkv_a", [P, 3, BATCH * SEQ])
        q_t = qkv_a[:, 0].rearrange("p (b s) -> p b s", b=BATCH)
        k_t = qkv_a[:, 1].rearrange("p (b s) -> p b s", b=BATCH)
        v_a = qkv_a[:, 2].rearrange("p (t d) -> p t d", t=TILES)
        rot = sb("rot", [P, 2, CHUNK])
        mx = sb("mx", [P, TILES])
        nmx = sb("nmx", [P, TILES])
        rsum = sb("rsum", [P, TILES])
        rinv = sb("rinv", [P, TILES])
        probs = sb("probs", [P, 2, SEQ])
        probs_t = sb("probs_t", [P, 2, SEQ])
        y_a = sb("y_a", [P, BATCH * BT, P])
        w_12 = sb("w_12", [P, 2, HID])
        w_hh = sb("w_hh", [P, 2, KT_, HID])
        w_h1, w_h2 = w_hh[:, 0], w_hh[:, 1]
        w_3 = sb("w_3", [P, KT_, P])
        s_b = sb("s_b", [P, 16])
        s_3 = sb("s_3", [P, P])
        sg = rot
        hid = sb("hid", [P, 3, KT_, CHUNK])
        w_c = sb("w_c", [P, 3 * P])
        w_o = sb("w_o", [P, P])
        w_os = sb("w_os", [P, P])
        b_o = sb("b_o", [P, P])
        sm = sb("sm", [P, SM_W])
        tiny = sb("tiny", [P, 64])
        nlam = sb("nlam", [P, 1])
        cs_tab = sb("cs_tab", [P, 2, HEADS, CT, 2])
        raw = sb("raw", [P, 2, HEADS, CT * VH])
        sq = sb("sq", [P, 2, HEADS, CT * VH])
        ss = sb("ss", [P, P])
        part = [sb(f"part{i}", [P, 2, BATCH * HEADS, BT * VH], BF16) for i in range(3)]
        v_c = sb("v_c", [P, BATCH * HEADS, BT, VH])
        u_q = sb("u_q", [P, 2, BT, P], BF16)
        u_k = sb("u_k", [P, 2, BT, P], BF16)
        q_s = sb("q_s", [P, 2, SEQ], BF16)
        k_s = sb("k_s", [P, 2, SEQ], BF16)
        k_1 = sb("k_1", [P, 2, SEQ], BF16)
        k_2 = sb("k_2", [P, 2, SEQ], BF16)
        v_h = sb("v_h", [P, 2, BT, VW])
        gain = sb("gain", [P, 2])
        gg = probs
        flat_hid = hid[:].rearrange("p a b c -> p (a b c)")
        zz = flat_hid[:, 0:4 * SEQ].rearrange("p (a b) -> p a b", a=2)
        ee = w_hh[:].rearrange("p a b c -> p (a b c)").rearrange("p (a b) -> p a b", a=2)
        acc_sb = w_12[:, 0]
        flat_a = qkv_a[:].rearrange("p a b -> p (a b)")
        o_size = BATCH * HEADS * CT * 4 * (VH + 1)
        o_all = flat_a[:, 0:o_size].rearrange("p (n c g v) -> p n c g v", n=BATCH * HEADS, c=CT, g=4)
        xt_d = [xt[:], xt_c[:]] + [flat_a[:, o_size + i * CHUNK:o_size + (i + 1) * CHUNK] for i in range(2)]
        r_o = sb("r_o", [P, 2, 2, HEADS * CT])
        ms_o = sb("ms_o", [P, 2, HEADS * CT])
        t_o = [w.rearrange("p (a n v) -> p a n v", a=2, v=VH) for w in
               (probs_t[:, 1], y_a[:, 2 * CT:].rearrange("p a b -> p (a b)"))]
        y_c = [xn_c, sb("y_c1", [P, CT, P])]
        y_ct = w_12[:, 1]
        w_g = tab[:, 0].rearrange("p (e i) -> p e i", e=EXPERTS)
        w_u = tab[:, 1].rearrange("p (e i) -> p e i", e=EXPERTS)
        w_d = probs_t[:, 0].rearrange("p (e i) -> p e i", e=EXPERTS)
        w_r = sb("w_r", [P, EXPERTS])
        rt = w_a[:].rearrange("p a b -> p (a b)")[:, 0:8 * BT * EXPERTS].rearrange("p (a t e) -> p a t e", a=8, t=BT)
        pair = raw[:].rearrange("p a h v -> p (a h v)").rearrange("p (a t e f) -> p a t e f", a=2, t=BT, e=EXPERTS)
        rs1 = sb("rs1", [P, 4, BT])
        wts = sb("wts", [P, BATCH, BT, EXPERTS])
        sg_d, h_d = (flat_hid[:, 2 * CHUNK * i:2 * CHUNK * (i + 1)].rearrange("p (a b) -> p a b", a=2)
                     for i in range(2))
        e_out = flat_hid[:, 4 * CHUNK:6 * CHUNK].rearrange("p (a b c) -> p a b c", a=2, b=CT)
        gains = sb("gains", [P, BATCH * HEADS])

        ps = ctx.enter_context(nc.psum_tensor("ps", [P, 8, CHUNK], F32))
        turn = ps[:, BANK_TURN, :]
        turn_bf = turn.bitcast(BF16)

        ld = {n: sem(f"ld_{n}") for n in ("x0", "x1", "x2", "x3", "aw", "tab", "idf", "con", "bw", "bh", "cw", "dw")}
        s_self = {n: sem(f"self_{n}") for n in ("dve", "pool", "act")}
        names = """stats rstd
            xn_a tp_a xt_a qp_a kp_a v_a rq1 rk1 rq2 rk2 ropeq ropek vout
            s_a m_a e_a pt_a pe_a o_a y_a
            xn_b tp_b xt_b gu_b sg_b h_b m1_b g1_b m2_b g2_b y_b yo_b
            xn_c tp_c xt_c qkv_c raw_c vraw_c sq_c rs_c qh_c hi_c r1_c mid_c lo_c
            small_c fact_c
            uq uk vh gcp turned turn_read k12 dd l1 l2 g z1 z2 e av accout
            ro to_a ms_o yc ytp yt wo wo_read xn_d tp_d xt_d rt_d z_d tanh_d dist_d ex_d
            gu_d sg_d h_d eo_d sc_d ad_d xfin stored""".split()
        S = {n: sem("e_" + n) for n in names}

        block = ctx.enter_context(nc.Block())

        x_src = x_in.rearrange("b (j p) d -> p (b j) d", p=P)
        out_dst = out.rearrange("b (j p) d -> p (b j) d", p=P)

        def chunk(c):
            return slice(c * CT, c * CT + CT)

        banks = ps[:].rearrange("p a b -> p (a b)")

        def part_at(c):
            b, half = divmod(c, 2)
            return (slice(None), slice(None), slice(b * HEADS, (b + 1) * HEADS),
                    slice(half * CT * VH, (half + 1) * CT * VH))

        def att_width(i):
            return min(P * (i + 1) + 1, SEQ)

        def y_d(c):
            return y_a[:, (c % 2) * CT:(c % 2) * CT + CT, :]

        def c_table(dve, v, me):
            dve.wait_ge(S["fact_c"], 1)
            me.step(v.tensor_tensor(tiny[:, 48:49], tiny[:, 1:2], tiny[:, 0:1], ALU.subtract))
            me.mark(v.tensor_scalar(nlam[:], tiny[:, 48:49], -LAMBDA_INIT, None, ALU.add))
            me.mark(v.tensor_scalar(tiny[:, 49:50], tiny[:, 16:17], COS_MAX / 2, COS_MAX / 2, ALU.mult, ALU.add))
            me.step(v.tensor_scalar(tiny[:, 8:16], tiny[:, 8:16], 0.5, 1.0, ALU.mult, ALU.add))
            me.step(v.tensor_scalar(tiny[:, 8:16], tiny[:, 8:16], tiny[:, 49:50], None, ALU.mult))
            me.mark(v.tensor_copy(cs_tab[:, 0].rearrange("p h k c -> p h (k c)"),
                                  tiny[:, 8:16].unsqueeze(2).to_broadcast([P, HEADS, 2 * CT])))
            me.mark(v.memset(cs_tab[:, 1, :, :, 0], 1.0))
            me.step(v.memset(cs_tab[:, 1, :, :, 1], -1.0))

        @block.sync
        def _(sp):
            sp.dma_start(x[:, chunk(0), :], x_src[:, chunk(0), :]).then_inc(ld["x0"], 16)
            sp.dma_start(ident[:], ident_in).then_inc(ld["idf"], 16)
            sp.dma_start(w_a[:].rearrange("p a b -> p (a b)"), a_w).then_inc(ld["aw"], 16)
            sp.dma_start(x[:, chunk(1), :], x_src[:, chunk(1), :]).then_inc(ld["x1"], 16)
            sp.dma_start(tab[:], rope).then_inc(ld["tab"], 16)
            for c in range(2, CHUNKS):
                sp.dma_start(x[:, chunk(c), :], x_src[:, chunk(c), :]).then_inc(ld[f"x{c}"], 16)
            sp.dma_start(ident_bf[:], ident_bf_in).then_inc(ld["con"], 16)
            sp.dma_start(mask[:], mask_in).then_inc(ld["con"], 16)
            sp.dma_start(w_12[:].rearrange("p a b -> p (a b)"), b_w12).then_inc(ld["bw"], 16)
            sp.dma_start(s_b[:], b_s).then_inc(ld["bw"], 16)
            sp.dma_start(s_3[:], b_s3).then_inc(ld["bw"], 16)
            sp.dma_start(w_h1[:], b_h1).then_inc(ld["bh"], 16)
            sp.dma_start(w_h2[:], b_h2).then_inc(ld["bh"], 16)
            sp.dma_start(w_3[:], b_w3).then_inc(ld["bh"], 16)
            sp.dma_start(w_c[:], c_w).then_inc(ld["cw"], 16)
            sp.dma_start(w_o[:], c_wo).then_inc(ld["cw"], 16)
            sp.dma_start(b_o[:], c_bo).then_inc(ld["cw"], 16)
            sp.dma_start(sm[:], small).then_inc(ld["cw"], 16)
            sp.wait_ge(S["rq2"], CHUNKS)
            sp.wait_ge(S["rk2"], CHUNKS)
            sp.wait_ge(S["o_a"], TILES)
            sp.dma_start(w_g[:], d_wg).then_inc(ld["dw"], 16)
            sp.dma_start(w_u[:], d_wu).then_inc(ld["dw"], 16)
            sp.dma_start(w_d[:], d_wd).then_inc(ld["dw"], 16)
            sp.dma_start(w_r[:], d_wr).then_inc(ld["dw"], 16)
            sp.dma_start(before[:].rearrange("p a b -> p (a b)"), before_in).then_inc(ld["dw"], 16)
            for c in range(CHUNKS):
                sp.wait_ge(S["xfin"], c + 1)
                sp.dma_start(out_dst[:, chunk(c), :], x[:, chunk(c), :]).then_inc(S["stored"], 16)
            sp.wait_ge(S["stored"], 16 * CHUNKS)

        @block.tensor
        def _(pe):
            mm = nc.tensor.matmul

            def turn_chunk(src):
                for k in range(CT):
                    last = nc.tensor.transpose(turn[:, k * P:(k + 1) * P], src[:, k, :], ident[:])
                return last

            def a_turn_x(c):
                pe.wait_ge(S["xn_a"], c + 1)
                pe.wait_ge(S["xt_a"], c)
                turn_chunk(xn_2[c % 2]).then_inc(S["tp_a"], 1)

            pe.wait_ge(ld["idf"], 16)
            a_turn_x(0)
            pe.wait_ge(ld["aw"], 16)
            for c in range(CHUNKS):
                src = (xt, xt_c)[c % 2]
                pe.wait_ge(S["xt_a"], c + 1)
                pe.wait_ge(S["rq2"], c)
                mm(ps[:, 0, :], w_a[:, 0, :], src[:], start=True, stop=True)
                mm(ps[:, 1, :], w_a[:, 1, :], src[:], start=True, stop=True).then_inc(S["qp_a"], 1)
                pe.wait_ge(S["rk2"], c)
                mm(ps[:, 2, :], w_a[:, 2, :], src[:], start=True, stop=True)
                mm(ps[:, 3, :], w_a[:, 3, :], src[:], start=True, stop=True).then_inc(S["kp_a"], 1)
                if c + 1 < CHUNKS:
                    a_turn_x(c + 1)
                pe.wait_ge(S["vout"], c)
                for k in range(CT):
                    last = mm(ps[:, 4, k * P:(k + 1) * P], src[:, k * P:(k + 1) * P], w_a[:, 4, :],
                              start=True, stop=True)
                last.then_inc(S["v_a"], 1)

            def a_scores(t):
                b, i = divmod(t, BT)
                base = 2 * (t % 2)
                if t == 0:
                    pe.wait_ge(ld["con"], 32)
                    pe.wait_ge(S["rq2"], CHUNKS)
                    pe.wait_ge(S["rk2"], CHUNKS)
                pe.wait_ge(S["ropeq"], 2 * b + 2)
                pe.wait_ge(S["ropek"], 2 * b + 2)
                if t >= 2:
                    pe.wait_ge(S["e_a"], t - 1)
                w = att_width(i)
                for n0 in range(0, w, CHUNK):
                    n1 = min(w, n0 + CHUNK)
                    m0, m1 = max(n0, P * i), n1
                    bank = base + n0 // CHUNK
                    masked = m1 > m0
                    last = mm(ps[:, bank, 0:n1 - n0], q_t[:, b, i * P:(i + 1) * P], k_t[:, b, n0:n1],
                              start=True, stop=not masked)
                    if masked:
                        last = mm(ps[:, bank, m0 - n0:m1 - n0], ident_bf[:],
                                  mask[:, m0 - P * i:m1 - P * i], start=False, stop=True)
                last.then_inc(S["s_a"], 1)

            def a_turn(t):
                i = t % BT
                pe.wait_ge(S["e_a"], t + 1)
                if t == 0:
                    pe.wait_ge(S["vout"], CHUNKS)
                pe.wait_ge(S["pe_a"], t)
                for j in range(i + 1):
                    last = nc.tensor.transpose(ps[:, 4 + j // CT, (j % CT) * P:(j % CT + 1) * P],
                                               probs[:, t % 2, j * P:(j + 1) * P], ident[:])
                if i < BT - 1:
                    j = i + 1
                    last = nc.tensor.transpose(ps[0:1, 4 + j // CT, (j % CT) * P:(j % CT + 1) * P],
                                               probs[:, t % 2, j * P:j * P + 1], ident[:])
                last.then_inc(S["pt_a"], 1)

            def a_values(t):
                b, i = divmod(t, BT)
                pe.wait_ge(S["pe_a"], t + 1)
                if t >= 2:
                    pe.wait_ge(S["y_a"], t - 1)
                if t == 1:
                    pe.wait_ge(S["xt_a"], CHUNKS)
                o = ps[:, 6 + t % 2, 0:P]
                for j in range(i + 1):
                    last = mm(o, probs_t[:, t % 2, j * P:(j + 1) * P], v_a[:, b * BT + j, :],
                              start=(j == 0), stop=(i == BT - 1 and j == i))
                if i < BT - 1:
                    j = i + 1
                    last = mm(o, probs_t[0:1, t % 2, j * P:(j + 1) * P], v_a[0:1, b * BT + j, :],
                              start=False, stop=True)
                last.then_inc(S["o_a"], 1)

            for t in range(TILES + 2):
                if t < TILES:
                    a_scores(t)
                if 1 <= t <= TILES:
                    a_turn(t - 1)
                if t >= 2:
                    a_values(t - 2)

            def b_turn(c):
                pe.wait_ge(S["xn_b"], c + 1)
                pe.wait_ge(S["xt_b"], c)
                if c >= 3:
                    pe.wait_ge(S["xt_c"], c - 2)
                turn_chunk(xn).then_inc(S["tp_b"], 1)

            def c_prep(c):
                pe.wait_ge(S["xn_c"], c + 1)
                pe.wait_ge(S["xt_b"], min(c + 3, CHUNKS))
                turn_chunk(xn_c).then_inc(S["tp_c"], 1)
                pe.wait_ge(S["xt_c"], c + 1)
                if c == 0:
                    pe.wait_ge(ld["cw"], 64)
                for k in range(CT):
                    if CT * c + k >= 2:
                        pe.wait_ge(S["vraw_c"], CT * c + k - 1)
                    mm(ps[:, 5 + k % 2, 0:3 * P], xt_c[:, k * P:(k + 1) * P], w_c[:],
                       start=True, stop=True).then_inc(S["qkv_c"], 1)

            pe.wait_ge(S["y_a"], TILES)
            b_turn(0)
            pe.wait_ge(ld["bw"], 48)
            for c in range(CHUNKS):
                pe.wait_ge(S["xt_b"], c + 1)
                for m in range(KT_):
                    if m >= 2:
                        pe.wait_ge(S["h_b"], KT_ * c + m - 1)
                    elif c >= 1:
                        pe.wait_ge(S["g2_b"], KT_ * c)
                    for w in range(2):
                        last = mm(ps[:, 2 * (m % 2) + w, :], w_12[:, w, m * P:(m + 1) * P], xt[:],
                                  start=True, stop=True)
                    last.then_inc(S["gu_b"], 1)
                if c == 0:
                    pe.wait_ge(ld["bh"], 48)
                for o in range(KT_):
                    if o == 0:
                        pe.wait_ge(S["h_b"], KT_ * c + 3)
                    if o == 2:
                        pe.wait_ge(S["h_b"], KT_ * c + 4)
                    for k in range(KT_):
                        if o == 0 and k >= 2:
                            pe.wait_ge(S["h_b"], KT_ * c + k + 1)
                        last = mm(ps[:, o, :], w_h1[:, k, o * P:(o + 1) * P], hid[:, 0, k, :],
                                  start=(k == 0), stop=(k == KT_ - 1))
                    last.then_inc(S["m1_b"], 1)
                if c + 1 < CHUNKS:
                    b_turn(c + 1)
                for o in range(KT_):
                    pe.wait_ge(S["g1_b"], KT_ * c + o + 1)
                    for k in range(KT_):
                        if o == 0:
                            pe.wait_ge(S["g1_b"], KT_ * c + k + 1)
                        last = mm(ps[:, o, :], w_h2[:, k, o * P:(o + 1) * P], hid[:, 1, k, :],
                                  start=(k == 0), stop=(k == KT_ - 1))
                    last.then_inc(S["m2_b"], 1)
                if c >= 1:
                    c_prep(c - 1)
                pe.wait_ge(S["yo_b"], c)
                for k4 in range(CT):
                    for k in range(KT_):
                        if k4 == 0:
                            pe.wait_ge(S["g2_b"], KT_ * c + k + 1)
                        last = mm(ps[:, 4, k4 * P:(k4 + 1) * P], hid[:, 2, k, k4 * P:(k4 + 1) * P],
                                  w_3[:, k, :], start=(k == 0), stop=(k == KT_ - 1))
                last.then_inc(S["y_b"], 1)

            def c_turning(use):
                kind, i = use
                pe.wait_ge(S["turn_read"], turns_done(use) - 1)
                if kind in "kq":
                    src, ready = (u_q, "uq") if kind == "q" else (u_k, "uk")
                    pe.wait_ge(S[ready], i + 1)
                    for j in range(BT):
                        last = nc.tensor.transpose(turn_bf[:, j * P:(j + 1) * P], src[:, i % 2, j, :], ident_bf[:])
                elif kind == "o":
                    pe.wait_ge(S["accout"], i + 1)
                    last = turn_chunk(acc_sb.rearrange("p (a b) -> p a b", a=CT))
                elif kind == "late turn":
                    pe.wait_ge(S["xn_c"], CHUNKS)
                    last = turn_chunk(xn_c)
                elif kind == "late qkv":
                    last = mm(turn[:, 0:3 * P], xt_c[:, i * P:(i + 1) * P], w_c[:], start=True, stop=True)
                elif kind == "y":
                    pe.wait_ge(S["yc"], i + 1)
                    last = turn_chunk(y_c[i % 2])
                elif kind == "wo":
                    if i == 0:
                        pe.wait_ge(S["small_c"], 1)
                    for k in range(CT):
                        last = mm(turn[:, k * P:(k + 1) * P], y_ct[:, k * P:(k + 1) * P], w_os[:],
                                  start=True, stop=True)
                elif kind == "x":
                    pe.wait_ge(S["xn_d"], i + 1)
                    last = turn_chunk(xn)
                else:
                    if i == 0:
                        pe.wait_ge(ld["dw"], 80)
                    last = router(i, turn)
                last.then_inc(S["turned"], 1)

            def router(c, bank, col=0):
                for k in range(CT):
                    o = col + k * EXPERTS
                    last = mm(bank[:, o:o + EXPERTS], xt_d[c][:, k * P:(k + 1) * P], w_r[:], start=True, stop=True)
                return last

            def c_scores(s, u, mt):
                keys = slice(mt * P, (mt + 1) * P)
                for base, k_op, free, done in ((0, k_s, "g", "dd"), (2, k_1, "z1", "l1"), (4, k_2, "z2", "l2")):
                    pe.wait_ge(S[free], s)
                    for half in range(2):
                        last = mm(ps[:, base + half, :], k_op[:, u, keys],
                                  q_s[:, u, half * CHUNK:(half + 1) * CHUNK], start=True, stop=True)
                    last.then_inc(S[done], 1)

            def c_values(s, u, mt):
                pe.wait_ge(S["e"], s + 1)
                for g4 in range(4):
                    last = mm(ps[VW * g4:VW * g4 + VW, 6, :], v_h[:, u, mt, :],
                              ee[:, mt % 2, g4 * CHUNK:(g4 + 1) * CHUNK],
                              start=(mt == 0), stop=(mt == BT - 1), skip_group_check=True)
                last.then_inc(S["av"], 1)

            pe.wait_ge(S["xt_c"], CHUNKS - 1)
            pe.wait_ge(S["vraw_c"], TILES - CT)
            c_turning(("k", 0))
            c_turning(("q", 0))
            pe.wait_ge(S["turn_read"], turns_done(("q", 0)))
            pe.wait_ge(S["k12"], 1)
            pe.wait_ge(S["yo_b"], CHUNKS)
            c_scores(0, 0, 0)
            c_scores(1, 0, 1)
            for n in range(NH):
                u = n % 2
                for mt in range(BT):
                    s = n * BT + mt
                    if mt < BT - 2:
                        c_scores(s + 2, u, mt + 2)
                    elif n < NH - 1:
                        if mt == BT - 2:
                            pe.wait_ge(S["k12"], n + 2)
                            pe.wait_ge(S["turn_read"], turns_done(("q", n + 1)))
                        c_scores(s + 2, 1 - u, mt + 2 - BT)
                    if mt == 0:
                        pe.wait_ge(S["vh"], n + 1)
                        pe.wait_ge(S["accout"], n)
                    c_values(s, u, mt)
                    use = turning(n, mt)
                    if use:
                        c_turning(use)
            c_turning(("o", NH - 1))

            def d_up(c, e):
                n = EXPERTS * c + e
                if n >= 2:
                    pe.wait_ge(S["h_d"], n - 1)
                if c >= 2 and e == 0:
                    pe.wait_ge(S["xt_d"], c - 1)
                for w, wt in enumerate((w_g, w_u)):
                    last = mm(ps[:, 2 * (e % 2) + w, :], wt[:, e, :], xt_d[c], start=True, stop=True)
                last.then_inc(S["gu_d"], 1)

            def d_down(c, e):
                n = EXPERTS * c + e
                pe.wait_ge(S["h_d"], n + 1)
                if n >= 2:
                    pe.wait_ge(S["sc_d"], n - 1)
                for k in range(CT):
                    last = mm(ps[:, 4 + e % 2, k * P:(k + 1) * P], h_d[:, e % 2, k * P:(k + 1) * P],
                              w_d[:, e, :], start=True, stop=True)
                last.then_inc(S["eo_d"], 1)

            def d_turn_y(c):
                pe.wait_ge(S["yc"], c + 1)
                if c > 2:
                    pe.wait_ge(S["yt"], c - 2)
                turn_chunk(y_c[c % 2]).then_inc(S["ytp"], 1)

            def d_wo(c):
                pe.wait_ge(S["yt"], c - 1)
                if c > 2:
                    pe.wait_ge(S["wo_read"], c - 2)
                for k in range(CT):
                    last = mm(ps[:, 6, k * P:(k + 1) * P], y_ct[:, k * P:(k + 1) * P], w_os[:], start=True, stop=True)
                last.then_inc(S["wo"], 1)

            def d_turn_x(c):
                pe.wait_ge(S["xn_d"], c + 1)
                pe.wait_ge(S["yt"], 2)
                if c > 2:
                    pe.wait_ge(S["xt_d"], c - 2)
                turn_chunk(xn).then_inc(S["tp_d"], 1)

            def d_route(c):
                pe.wait_ge(S["xt_d"], c - 1)
                pe.wait_ge(S["wo_read"], 2)
                router(c, ps[:, 6, :], (c - 2) * CT * EXPERTS).then_inc(S["rt_d"], 1)

            pe.wait_ge(S["turn_read"], len(TURNS))
            for c in range(CHUNKS):
                for e in range(EXPERTS):
                    d_up(c, e)
                    if e >= 1:
                        d_down(c, e - 1)
                    if (c, e) in ((0, 6), (1, 0)):
                        d_turn_y(2 + c)
                    if (c, e) in ((0, 7), (1, 1)):
                        d_wo(2 + c)
                    if (c, e) in ((1, 5), (1, 7)):
                        d_turn_x(2 + (e == 7))
                    if (c, e) == (1, 6):
                        d_route(2)
                d_down(c, EXPERTS - 1)
                if c == 1:
                    d_route(3)

        @block.scalar
        def _(act):
            A = nc.scalar.activation
            me = Turn(act, s_self["act"])

            def a_xt(c):
                act.wait_ge(S["tp_a"], c + 1)
                if c >= 2:
                    act.wait_ge(S["v_a"], c - 1)
                A((xt, xt_c)[c % 2][:], turn, ACT.Copy).then_inc(S["xt_a"], 1)

            a_xt(0)
            for c in range(CHUNKS):
                if c + 1 < CHUNKS:
                    a_xt(c + 1)
                act.wait_ge(S["v_a"], c + 1)
                A(v_a[:, chunk(c), :].rearrange("p a b -> p (a b)"), ps[:, 4, :], ACT.Copy).then_inc(S["vout"], 1)

            def a_exp(t):
                w = att_width(t % BT)
                act.wait_ge(S["m_a"], t + 1)
                if t >= 2:
                    act.wait_ge(S["pt_a"], t - 1)
                base = 2 * CHUNK * (t % 2)
                A(probs[:, t % 2, 0:w], banks[:, base:base + w], ACT.Exp, bias=nmx[:, t:t + 1],
                  scale=ATT_SCALE, accum_out=rsum[:, t:t + 1]).then_inc(S["e_a"], 1)

            def a_turned(t):
                i = t % BT
                act.wait_ge(S["pt_a"], t + 1)
                if t >= 2:
                    act.wait_ge(S["o_a"], t - 1)
                w = P * (i + 1)
                src = banks[:, 4 * CHUNK:6 * CHUNK]
                last = A(probs_t[:, t % 2, 0:w], src[:, 0:w], ACT.Copy)
                if i < BT - 1:
                    last = A(probs_t[0:1, t % 2, w:w + P], src[0:1, w:w + P], ACT.Copy)
                last.then_inc(S["pe_a"], 1)

            for t in range(TILES + 1):
                if t < TILES:
                    a_exp(t)
                if t >= 1:
                    a_turned(t - 1)

            def b_xt(c):
                act.wait_ge(S["tp_b"], c + 1)
                act.wait_ge(S["gu_b"], KT_ * c)
                A(xt[:], turn, ACT.Copy).then_inc(S["xt_b"], 1)

            def c_evac(c):
                act.wait_ge(S["tp_c"], c + 1)
                act.wait_ge(S["qkv_c"], CT * c)
                A(xt_c[:], turn, ACT.Copy).then_inc(S["xt_c"], 1)
                b, half = divmod(c, 2)
                for k in range(CT):
                    act.wait_ge(S["qkv_c"], CT * c + k + 1)
                    if k == 0 and c:
                        act.wait_ge(S["lo_c"], c)
                    bank = ps[:, 5 + k % 2, :]
                    A(raw[:, :, :, k * VH:(k + 1) * VH],
                      bank[:, 0:2 * P].rearrange("p (a h v) -> p a h v", a=2, h=HEADS), ACT.Copy).then_inc(S["raw_c"], 1)
                    A(v_c[:, b * HEADS:(b + 1) * HEADS, half * CT + k, :],
                      bank[:, 2 * P:3 * P].rearrange("p (h v) -> p h v", h=HEADS), ACT.Copy).then_inc(S["vraw_c"], 1)

            def c_parts(c):
                act.wait_ge(S["qh_c"], c + 1)
                A(part[0][part_at(c)], sq[:], ACT.Copy).then_inc(S["hi_c"], 1)
                act.wait_ge(S["r1_c"], c + 1)
                A(part[1][part_at(c)], raw[:], ACT.Copy).then_inc(S["mid_c"], 1)

            b_xt(0)
            act.wait_ge(ld["bw"], 48)
            for c in range(CHUNKS):
                for m in range(KT_):
                    n = KT_ * c + m
                    act.wait_ge(S["gu_b"], n + 1)
                    if n >= 2:
                        act.wait_ge(S["h_b"], n - 1)
                    A(sg[:, m % 2, :], ps[:, 2 * (m % 2), :], ACT.Silu, scale=s_b[:, m:m + 1]).then_inc(S["sg_b"], 1)
                for o in range(KT_):
                    act.wait_ge(S["m1_b"], KT_ * c + o + 1)
                    if c:
                        act.wait_ge(S["m2_b"], KT_ * c)
                    A(hid[:, 1, o, :], ps[:, o, :], ACT.Gelu, scale=s_b[:, 8 + o:9 + o]).then_inc(S["g1_b"], 1)
                if c + 1 < CHUNKS:
                    b_xt(c + 1)
                if c >= 2:
                    c_parts(c - 2)
                for o in range(KT_):
                    act.wait_ge(S["m2_b"], KT_ * c + o + 1)
                    if c:
                        act.wait_ge(S["y_b"], c)
                    A(hid[:, 2, o, :], ps[:, o, :], ACT.Gelu, scale=s_b[:, 12 + o:13 + o]).then_inc(S["g2_b"], 1)
                if c == 0:
                    act.wait_ge(S["small_c"], 1)
                    me.step(A(tiny[:, 0:2], tiny[:, 0:2], ACT.Exp))
                    A(tiny[:, 8:17], tiny[:, 8:17], ACT.Tanh).then_inc(S["fact_c"], 1)
                if c >= 1:
                    c_evac(c - 1)

            def tanh_step(s, u, mt):
                act.wait_ge(S["dd"], s + 1)
                if s >= 2:
                    act.wait_ge(S["z2"], s - 1)
                A(gg[:, mt % 2, :], banks[:, 0:2 * CHUNK], ACT.Tanh, scale=gain[:, u:u + 1]).then_inc(S["g"], 1)

            act.wait_ge(S["gcp"], 1)
            tanh_step(0, 0, 0)
            for n in range(NH):
                u = n % 2
                for mt in range(BT):
                    s = n * BT + mt
                    if mt < BT - 1:
                        tanh_step(s + 1, u, mt + 1)
                    elif n < NH - 1:
                        act.wait_ge(S["gcp"], n + 2)
                        tanh_step(s + 1, 1 - u, 0)
                    act.wait_ge(S["z2"], s + 1)
                    if s == NH * BT - 1:
                        act.wait_ge(S["av"], s - 1)
                    A(ee[:, mt % 2, :], zz[:, mt % 2, :], ACT.Exp).then_inc(S["e"], 1)

            def d_gate(b):
                if b == 0:
                    act.wait_ge(S["turn_read"], turns_done(("route", 1)))
                else:
                    act.wait_ge(S["z_d"], 2)
                A(rt[:, 1], rt[:, 0], ACT.Tanh, scale=0.5).then_inc(S["tanh_d"], 1)

            def d_exps(b):
                act.wait_ge(S["dist_d"], b + 1)
                me.mark(A(rt[:, 3], rt[:, 2], ACT.Exp, scale=-1.0 / 0.1))
                A(rt[:, 4], rt[:, 2], ACT.Exp, scale=-1.0 / 0.3).then_inc(S["ex_d"], 1)

            def d_yt(c):
                act.wait_ge(S["ytp"], c - 1)
                if c > 2:
                    act.wait_ge(S["wo"], c - 2)
                A(y_ct, turn, ACT.Copy).then_inc(S["yt"], 1)

            def d_xt(c):
                act.wait_ge(S["tp_d"], c - 1)
                A(xt_d[c], turn, ACT.Copy).then_inc(S["xt_d"], 1)

            d_gate(0)
            d_exps(0)
            for c in range(CHUNKS):
                for e in range(EXPERTS):
                    n = EXPERTS * c + e
                    act.wait_ge(S["gu_d"], n + 1)
                    if n >= 2:
                        act.wait_ge(S["h_d"], n - 1)
                    A(sg_d[:, e % 2, :], ps[:, 2 * (e % 2), :], ACT.Silu).then_inc(S["sg_d"], 1)
                    if (c, e) in ((0, 6), (1, 0)):
                        d_yt(2 + c)
                    if (c, e) in ((1, 5), (1, 7)):
                        d_xt(2 + (e == 7))
                    if (c, e) == (2, 0):
                        d_exps(1)
                if c == 1:
                    d_gate(1)

        @block.vector
        def _(dve):
            v = nc.vector
            me = Turn(dve, s_self["dve"])

            def rsqrt_start(dst, w):
                me.mark(v.tensor_scalar(nh[:, 0:w], nv[:, 0:w], -0.5, None, ALU.mult))
                me.step(v.tensor_scalar(dst.bitcast(I32), nv[:, 0:w].bitcast(I32), -0.5, RSQRT_MAGIC,
                                        ALU.mult, ALU.add))

            def rsqrt_newton(dst, w, done=None):
                t = nt[:, 0:w]
                me.step(v.tensor_tensor(t, dst, dst, ALU.mult))
                me.step(v.tensor_tensor(t, t, nh[:, 0:w], ALU.mult))
                last = v.scalar_tensor_tensor(dst, t, 1.5, dst, ALU.add, ALU.mult)
                if done:
                    last.then_inc(S[done], 1)
                else:
                    me.step(last)

            def stats(kind, c, src):
                i = NORMS.index((kind, c))
                if i >= 2:
                    dve.wait_ge(S["stats"], i - 1)
                for k in range(CT):
                    me.mark(v.bn_stats(st[:, i % 2, k, :], src[:, k, :]))
                me.wait()
                for k in range(CT):
                    last = v.bn_aggr(mv[:, i, k, :], st[:, i % 2, k, :])
                last.then_inc(S["stats"], 1)

            def apply(kind, c, src, dst, done=None):
                i = NORMS.index((kind, c))
                dve.wait_ge(S["rstd"], i + 1)
                for k in range(CT):
                    last = v.tensor_scalar(dst[:, k, :], src[:, k, :], mv[:, i, k, 0:1], rs[:, i, k:k + 1],
                                           ALU.subtract, ALU.mult)
                if done:
                    last.then_inc(S[done], 1)
                else:
                    me.step(last)

            def add_out(kind, c, src, done=None):
                apply(kind, c, src, src)
                last = v.tensor_tensor(x[:, chunk(c), :], x[:, chunk(c), :], src, ALU.add)
                if done:
                    last.then_inc(S[done], 1)
                else:
                    me.step(last)

            def x_of(c):
                return x[:, chunk(c), :]

            def a_apply(c):
                if c >= 2:
                    dve.wait_ge(S["tp_a"], c - 1)
                apply("a_in", c, x_of(c), xn_2[c % 2][:], "xn_a")

            def a_stats(c):
                dve.wait_ge(ld[f"x{c}"], 16)
                stats("a_in", c, x_of(c))

            a_stats(0)
            a_stats(1)
            a_apply(0)
            for c in range(CHUNKS):
                if c + 2 < CHUNKS:
                    a_stats(c + 2)
                if c + 1 < CHUNKS:
                    a_apply(c + 1)
                if c == 0:
                    dve.wait_ge(ld["tab"], 16)
                b, half = divmod(c, 2)
                at = slice(half * CHUNK, (half + 1) * CHUNK)
                for i, (dst, bank, got, r1, r2, summed) in enumerate(
                        ((q_t, 0, "qp_a", "rq1", "rq2", "ropeq"), (k_t, 2, "kp_a", "rk1", "rk2", "ropek"))):
                    dve.wait_ge(S[got], c + 1)
                    v.tensor_tensor(dst[:, b, at], ps[:, bank, :], tab[:, 0, at], ALU.mult).then_inc(S[r1], 1)
                    dve.wait_ge(S[summed], c)
                    v.tensor_tensor(rot[:, i, :], ps[:, bank + 1, :], tab[:, 1, at], ALU.mult).then_inc(S[r2], 1)

            def a_max(t):
                w = att_width(t % BT)
                dve.wait_ge(S["s_a"], t + 1)
                base = 2 * CHUNK * (t % 2)
                me.step(v.tensor_reduce(mx[:, t:t + 1], banks[:, base:base + w], AX.X, ALU.max))
                v.tensor_scalar(nmx[:, t:t + 1], mx[:, t:t + 1], -ATT_SCALE, None, ALU.mult).then_inc(S["m_a"], 1)

            def a_post(t):
                dve.wait_ge(S["e_a"], t + 1)
                me.step(v.reciprocal(rinv[:, t:t + 1], rsum[:, t:t + 1]))
                dve.wait_ge(S["o_a"], t + 1)
                v.tensor_scalar(y_a[:, t, :], ps[:, 6 + t % 2, 0:P], rinv[:, t:t + 1],
                                None, ALU.mult).then_inc(S["y_a"], 1)

            for t in range(TILES + 2):
                if t < TILES:
                    a_max(t)
                if t >= 2:
                    a_post(t - 2)
                if t >= 6 and t % CT == 2:
                    c = (t - 6) // CT
                    stats("a_out", c, y_a[:, chunk(c), :])
                if t >= 6 and t % CT == 3:
                    c = (t - 6) // CT
                    add_out("a_out", c, y_a[:, chunk(c), :])
                if t == 8:
                    stats("b_in", 0, x_of(0))
                if t == 9:
                    apply("b_in", 0, x_of(0), xn[:], "xn_b")
            dve.wait_ge(S["y_a"], TILES)
            stats("a_out", CHUNKS - 1, y_a[:, chunk(CHUNKS - 1), :])

            def b_hidden(c, m):
                n = KT_ * c + m
                if c:
                    dve.wait_ge(S["m1_b"], KT_ * c)
                dve.wait_ge(S["sg_b"], n + 1)
                v.scalar_tensor_tensor(hid[:, 0, m, :], ps[:, 2 * (m % 2) + 1, :], s_b[:, 4 + m:5 + m],
                                       sg[:, m % 2, :], ALU.mult, ALU.mult).then_inc(S["h_b"], 1)

            def b_y(c):
                dve.wait_ge(S["y_b"], c + 1)
                v.tensor_tensor(y[:], ps[:, 4, :].rearrange("p (a b) -> p a b", a=CT),
                                s_3[:].unsqueeze(1).to_broadcast([P, CT, P]), ALU.mult).then_inc(S["yo_b"], 1)
                dve.wait_ge(S["yo_b"], c + 1)
                stats("b_out", c, y[:])

            def c_const():
                dve.wait_ge(ld["cw"], 64)
                lam = sm[:, 0:32].rearrange("p (a c b) -> p a c b", a=2, c=2)
                me.step(v.tensor_tensor(tiny[:, 32:48].rearrange("p (a b) -> p a b", a=2),
                                        lam[:, :, 0, :], lam[:, :, 1, :], ALU.mult))
                me.mark(v.tensor_reduce(tiny[:, 0:2], tiny[:, 32:48].rearrange("p (a b) -> p a b", a=2), AX.X, ALU.add))
                me.step(v.tensor_reduce(tiny[:, 48:49], sm[:, SM_DELTA:SM_DELTA + HEADS], AX.X, ALU.add))
                me.step(v.tensor_scalar(tiny[:, 48:49], tiny[:, 48:49], 1.0 / HEADS, None, ALU.mult))
                me.mark(v.tensor_scalar(tiny[:, 8:16], sm[:, SM_DELTA:SM_DELTA + HEADS], tiny[:, 48:49], None, ALU.subtract))
                me.mark(v.tensor_scalar(tiny[:, 16:17], sm[:, SM_RAW:SM_RAW + 1], 0.5, None, ALU.mult))
                v.tensor_scalar(w_os[:], w_o[:], sm[:, SM_SUBLN:SM_SUBLN + 1], 1.0 - LAMBDA_INIT,
                                ALU.mult, ALU.mult).then_inc(S["small_c"], 1)

            def c_in(c):
                stats("c_in", c, x_of(c))

            def c_apply(c):
                if c:
                    dve.wait_ge(S["tp_c"], c)
                apply("c_in", c, x_of(c), xn_c[:], "xn_c")

            groups = "p a h (g d) -> p (a h g) d"

            def c_sums(c):
                dve.wait_ge(S["sq_c"], c + 1)
                me.step(v.tensor_reduce(ss[:], sq[:].rearrange(groups, d=DH), AX.X, ALU.add))
                me.step(v.tensor_scalar(nv[:], ss[:], 1e-12, 1e38, ALU.max, ALU.min))
                rsqrt_start(rstd[:], P)

            def c_factor():
                return v.tensor_tensor(rstd[:], rstd[:], cs_tab[:].rearrange("p a h k c -> p (a h k c)"), ALU.mult)

            def c_norms(c):
                c_sums(c)
                for _ in range(3):
                    rsqrt_newton(rstd[:], P)
                me.step(c_factor())
                v.tensor_tensor(sq[:].rearrange(groups, d=DH), raw[:].rearrange(groups, d=DH),
                                rstd[:].unsqueeze(2).to_broadcast([P, P, DH]), ALU.mult).then_inc(S["qh_c"], 1)
                dve.wait_ge(S["hi_c"], c + 1)
                v.tensor_tensor(raw[:], sq[:], part[0][part_at(c)], ALU.subtract).then_inc(S["r1_c"], 1)
                dve.wait_ge(S["mid_c"], c + 1)
                v.tensor_tensor(part[2][part_at(c)], raw[:], part[1][part_at(c)], ALU.subtract).then_inc(S["lo_c"], 1)

            dve.wait_ge(ld["bw"], 48)
            for c in range(CHUNKS):
                for m in range(KT_):
                    b_hidden(c, m)
                if c == 0:
                    add_out("a_out", CHUNKS - 1, y_a[:, chunk(CHUNKS - 1), :])
                else:
                    b_y(c - 1)
                if c + 1 < CHUNKS:
                    stats("b_in", c + 1, x_of(c + 1))
                if c:
                    add_out("b_out", c - 1, y[:])
                if c + 1 < CHUNKS:
                    dve.wait_ge(S["tp_b"], c + 1)
                    apply("b_in", c + 1, x_of(c + 1), xn[:], "xn_b")
                if c == 0:
                    c_const()
                else:
                    c_in(c - 1)
                if c == 1:
                    c_table(dve, v, me)
                if c >= 2:
                    c_norms(c - 2)
                if c:
                    c_apply(c - 1)
            b_y(CHUNKS - 1)

            def z_step(s, mt):
                dve.wait_ge(S["g"], s + 1)
                dve.wait_ge(S["l1"], s + 1)
                v.tensor_tensor(zz[:, mt % 2, 0:SEQ], banks[:, 2 * CHUNK:4 * CHUNK], gg[:, mt % 2, :],
                                ALU.add).then_inc(S["z1"], 1)
                dve.wait_ge(S["l2"], s + 1)
                v.scalar_tensor_tensor(zz[:, mt % 2, SEQ:2 * SEQ], banks[:, 4 * CHUNK:6 * CHUNK], -1.0,
                                       gg[:, mt % 2, :], ALU.mult, ALU.subtract).then_inc(S["z2"], 1)

            def turn_out(use):
                kind, i = use
                dve.wait_ge(S["turned"], turns_done(use))
                four = turn.rearrange("p (a b) -> p a b", a=CT)
                if kind == "k":
                    last = v.tensor_copy(k_s[:, i % 2, :], turn_bf)
                elif kind == "q":
                    last = v.tensor_copy(q_s[:, i % 2, :], turn_bf)
                elif kind == "o":
                    last = v.tensor_copy(o_flat[:, i, :, :], turn.rearrange("p (c w) -> p c w", w=VW)[:, :, 0:VH + 1])
                elif kind == "late turn":
                    dve.wait_ge(S["qkv_c"], TILES - CT)
                    last = v.tensor_copy(xt_c[:], turn)
                elif kind == "late qkv":
                    if i == 0:
                        dve.wait_ge(S["lo_c"], CHUNKS - 1)
                    b, half = divmod(CHUNKS - 1, 2)
                    v.tensor_copy(raw[:, :, :, i * VH:(i + 1) * VH],
                                  turn[:, 0:2 * P].rearrange("p (a h v) -> p a h v", a=2, h=HEADS)).then_inc(S["raw_c"], 1)
                    last = v.tensor_copy(v_c[:, b * HEADS:(b + 1) * HEADS, half * CT + i, :],
                                         turn[:, 2 * P:3 * P].rearrange("p (h v) -> p h v", h=HEADS))
                elif kind == "y":
                    last = v.tensor_copy(y_ct, turn)
                elif kind == "wo":
                    last = v.tensor_tensor(y[:], four, b_o[:].unsqueeze(1).to_broadcast([P, CT, P]), ALU.add)
                elif kind == "x":
                    last = v.tensor_copy(xt_d[i], turn)
                else:
                    last = logits(i, turn)
                last.then_inc(S["turn_read"], 1)

            o_flat = o_all[:].rearrange("p n c g v -> p n (c g) v")

            def k_halves(n, u):
                dve.wait_ge(S["turn_read"], turns_done(("k", n)))
                v.tensor_scalar(k_1[:, u, :], k_s[:, u, :], sm[:, SM_HALF:SM_HALF + 1], None, ALU.mult)
                v.tensor_scalar(k_2[:, u, :], k_s[:, u, :], sm[:, SM_HALF + 1:SM_HALF + 2], None,
                                ALU.mult).then_inc(S["k12"], 1)

            def acc_out(n):
                dve.wait_ge(S["av"], BT * (n + 1))
                if n:
                    dve.wait_ge(S["turned"], turns_done(("o", n - 1)))
                v.tensor_copy(acc_sb, ps[:, 6, :]).then_inc(S["accout"], 1)

            def heads_recip(b):
                dve.wait_ge(S["turn_read"], turns_done(("o", (b + 1) * HEADS - 1)))
                for half in range(2):
                    o = o_all[:, b * HEADS:(b + 1) * HEADS, :, :, :].rearrange("p h c g v -> p (h c) g v")
                    for comp in range(2):
                        me.mark(v.reciprocal(r_o[:, half, comp, :], o[:, :, 2 * comp + half, VH]))
                me.wait()
                v.tensor_scalar(r_o[:, :, 1, :], r_o[:, :, 1, :], nlam[:, 0:1], None, ALU.mult).then_inc(S["ro"], 1)

            W2 = 2 * HEADS * CT

            def heads_square(b):
                dve.wait_ge(S["to_a"], 2 * (b + 1))
                for half in range(2):
                    me.mark(v.tensor_reduce(ms_o[:, half, :], t_o[half][:, 1], AX.X, ALU.add))
                me.wait()
                me.step(v.tensor_scalar(nv[:, 0:W2], ms_o[:].rearrange("p a b -> p (a b)"), 1.0 / VH, RMS_EPS,
                                        ALU.mult, ALU.add))
                rsqrt_start(rstd[:, 0:W2], W2)

            def logits(half, src):
                return v.tensor_scalar(rt[:, 0, half * CT:(half + 1) * CT].rearrange("p a b -> p (a b)"),
                                       src[:, 0:CT * EXPERTS], rs1[:, 3, 0:1], None, ALU.mult)

            def route_a(b):
                dve.wait_ge(S["tanh_d"], b + 1)
                me.step(v.tensor_scalar(rt[:, 1], rt[:, 1], 0.5, 0.5, ALU.mult, ALU.add))
                me.step(v.tensor_scalar(rt[:, 5], rt[:, 1], -GOLDEN, None, ALU.add))
                v.scalar_tensor_tensor(rt[:, 2], rt[:, 5], -1.0, rt[:, 5], ALU.mult, ALU.max).then_inc(S["dist_d"], 1)
                me.mark(v.tensor_scalar(rt[:, 6], rt[:, 1], ZONE_LOW, None, ALU.is_ge))
                me.step(v.tensor_scalar(rt[:, 7], rt[:, 1], ZONE_HIGH, None, ALU.is_le))
                me.step(v.tensor_tensor(rt[:, 6], rt[:, 6], rt[:, 7], ALU.mult))

            def route_b(b):
                four = [P, BT, EXPERTS, EXPERTS]
                dve.wait_ge(S["ex_d"], b + 1)
                me.mark(v.tensor_tensor(rt[:, 3], rt[:, 3], rt[:, 6], ALU.mult))
                other = rt[:, 4].unsqueeze(2).to_broadcast(four)
                mine = rt[:, 4].unsqueeze(3).to_broadcast(four)
                me.mark(v.tensor_tensor(pair[:, 0], other, mine, ALU.is_gt))
                me.step(v.tensor_tensor(pair[:, 1], other, mine, ALU.is_equal))
                me.step(v.tensor_tensor(pair[:, 1], pair[:, 1], before[:].unsqueeze(1).to_broadcast(four), ALU.mult))
                me.step(v.tensor_tensor(pair[:, 0], pair[:, 0], pair[:, 1], ALU.add))
                me.step(v.tensor_reduce(rt[:, 5], pair[:, 0], AX.X, ALU.add))

            def route_c(b):
                w = wts[:, b]
                wide = [P, BT, EXPERTS]
                me.step(v.tensor_reduce(rs1[:, 0], rt[:, 3], AX.X, ALU.add))
                me.mark(v.scalar_tensor_tensor(rt[:, 7], rt[:, 5], 1.5, rt[:, 4], ALU.is_lt, ALU.mult))
                me.step(v.tensor_scalar(rs1[:, 1], rs1[:, 0], 1e-8, None, ALU.is_lt))
                me.step(v.tensor_reduce(rs1[:, 0], rt[:, 7], AX.X, ALU.add))
                me.step(v.tensor_scalar(rs1[:, 0], rs1[:, 0], 1e-8, None, ALU.max))
                me.step(v.reciprocal(rs1[:, 2], rs1[:, 0]))
                me.mark(v.tensor_tensor(rs1[:, 2], rs1[:, 2], rs1[:, 1], ALU.mult))
                me.step(v.tensor_scalar(rs1[:, 1], rs1[:, 1], -1.0, 1.0, ALU.mult, ALU.add))
                me.mark(v.tensor_tensor(rt[:, 3], rt[:, 3], rs1[:, 1].unsqueeze(2).to_broadcast(wide), ALU.mult))
                me.step(v.tensor_tensor(rt[:, 7], rt[:, 7], rs1[:, 2].unsqueeze(2).to_broadcast(wide), ALU.mult))
                me.step(v.tensor_tensor(rt[:, 3], rt[:, 3], rt[:, 7], ALU.add))
                me.step(v.tensor_reduce(rs1[:, 0], rt[:, 3], AX.X, ALU.add))
                me.step(v.tensor_scalar(rs1[:, 0], rs1[:, 0], 1e-8, None, ALU.max))
                me.step(v.reciprocal(rs1[:, 2], rs1[:, 0]))
                me.step(v.tensor_tensor(w, rt[:, 3], rs1[:, 2].unsqueeze(2).to_broadcast(wide), ALU.mult))

            turn_out(("k", 0))
            k_halves(0, 0)
            turn_out(("q", 0))
            c_sums(CHUNKS - 2)
            for n in range(NH):
                u = n % 2
                for mt in range(BT):
                    at = (n, mt)
                    z_step(n * BT + mt, mt)
                    use = turning(n, mt - 2) if mt >= 2 else turning(n - 1, 6) if mt == 0 and n else None
                    if use:
                        turn_out(use)
                    if mt == 1 and n:
                        acc_out(n - 1)
                    if mt == 3 and n < NH - 1:
                        k_halves(n + 1, 1 - u)
                    if at in ((0, 0), (0, 1), (0, 2)):
                        rsqrt_newton(rstd[:], P)
                    if at == (0, 2):
                        c_factor().then_inc(S["rs_c"], 1)
                    if at == (0, 0):
                        add_out("b_out", CHUNKS - 1, y[:])
                    if at == (0, 1):
                        c_in(CHUNKS - 1)
                    if at == (0, 2):
                        c_apply(CHUNKS - 1)
                    if at == (4, 5):
                        c_sums(CHUNKS - 1)
                    if at in ((4, 7), (5, 5), (5, 7)):
                        rsqrt_newton(rstd[:], P)
                    if at == (5, 7):
                        c_factor().then_inc(S["rs_c"], 1)
                    if at == (8, 7):
                        heads_recip(0)
                    if at == (9, 7):
                        heads_square(0)
                    if at in ((10, 1), (10, 3), (10, 5)):
                        rsqrt_newton(rstd[:, 0:W2], W2, "ms_o" if mt == 5 else None)
                    if at in ((12, 1), (14, 1)):
                        dve.wait_ge(S["turn_read"], turns_done(("wo", (n - 12) // 2)))
                        stats("c_out", (n - 12) // 2, y[:])
                    if at in ((12, 5), (14, 3)):
                        add_out("c_out", (n - 12) // 2, y[:])
                    if at in ((13, 1), (14, 5)):
                        stats("d_in", n - 13, x_of(n - 13))
                    if at == (13, 5):
                        apply("d_in", 0, x_of(0), xn[:], "xn_d")
                    if at == (15, 0):
                        dve.wait_ge(S["turned"], turns_done(("x", 0)))
                        apply("d_in", 1, x_of(1), xn[:], "xn_d")
                    if at == (14, 7):
                        dve.wait_ge(ld["dw"], 80)
                        me.step(v.reciprocal(rs1[:, 3, 0:1], sm[:, SM_TEMP:SM_TEMP + 1]))
            acc_out(NH - 1)
            turn_out(("route", 1))
            turn_out(("o", NH - 1))
            heads_recip(1)

            def d_hidden(c, e):
                n = EXPERTS * c + e
                dve.wait_ge(S["sg_d"], n + 1)
                if n >= 2:
                    dve.wait_ge(S["eo_d"], n - 1)
                v.tensor_tensor(h_d[:, e % 2, :], ps[:, 2 * (e % 2) + 1, :], sg_d[:, e % 2, :],
                                ALU.mult).then_inc(S["h_d"], 1)

            def d_scale(c, e):
                n = EXPERTS * c + e
                b, half = divmod(c, 2)
                dve.wait_ge(S["eo_d"], n + 1)
                if n >= 2:
                    dve.wait_ge(S["ad_d"], n - 1)
                v.tensor_tensor(e_out[:, e % 2], ps[:, 4 + e % 2, :].rearrange("p (a b) -> p a b", a=CT),
                                wts[:, b, half * CT:(half + 1) * CT, e].unsqueeze(2).to_broadcast([P, CT, P]),
                                ALU.mult).then_inc(S["sc_d"], 1)

            def wo_bias(c):
                dve.wait_ge(S["wo"], c - 1)
                v.tensor_tensor(y[:], ps[:, 6, :].rearrange("p (a b) -> p a b", a=CT),
                                b_o[:].unsqueeze(1).to_broadcast([P, CT, P]), ALU.add).then_inc(S["wo_read"], 1)
                dve.wait_ge(S["wo_read"], c - 1)

            def d_out_stats(c):
                dve.wait_ge(S["ad_d"], EXPERTS * (c + 1))
                stats("d_out", c, y_d(c))

            route_a(0)
            route_b(0)
            route_c(0)
            for c in range(CHUNKS):
                for e in range(EXPERTS):
                    at = (c, e)
                    d_hidden(c, e)
                    if at == (2, 0):
                        route_a(1)
                    if at == (2, 1):
                        route_b(1)
                    if at == (2, 2):
                        route_c(1)
                        d_scale(2, 0)
                    if e >= 1 and at != (2, 1):
                        d_scale(c, e - 1)
                    if at == (0, 3):
                        heads_square(1)
                        for i in range(3):
                            rsqrt_newton(rstd[:, 0:W2], W2, "ms_o" if i == 2 else None)
                    if at == (1, 0):
                        wo_bias(2)
                        stats("c_out", 2, y[:])
                    if at == (1, 1):
                        d_out_stats(0)
                    if at == (1, 2):
                        add_out("c_out", 2, y[:])
                        wo_bias(3)
                        stats("d_in", 2, x_of(2))
                        stats("c_out", 3, y[:])
                    if at == (1, 3):
                        dve.wait_ge(S["turned"], turns_done(("x", 1)))
                        apply("d_in", 2, x_of(2), xn[:], "xn_d")
                    if at == (1, 4):
                        add_out("c_out", 3, y[:])
                        stats("d_in", 3, x_of(3))
                    if at == (1, 5):
                        add_out("d_out", 0, y_d(0), "xfin")
                    if at == (1, 6):
                        dve.wait_ge(S["tp_d"], 1)
                        apply("d_in", 3, x_of(3), xn[:], "xn_d")
                    if c >= 2 and e == 1:
                        d_out_stats(c - 1)
                    if c >= 2 and e == 3:
                        add_out("d_out", c - 1, y_d(c - 1), "xfin")
                d_scale(c, EXPERTS - 1)
                if c == 1:
                    dve.wait_ge(S["rt_d"], 2)
                    for half in range(2):
                        logits(half, ps[:, 6, half * CT * EXPERTS:(half + 1) * CT * EXPERTS]).then_inc(S["z_d"], 1)
            d_out_stats(CHUNKS - 1)
            add_out("d_out", CHUNKS - 1, y_d(CHUNKS - 1), "xfin")

        @block.gpsimd
        def _(pool):
            g = nc.gpsimd
            me = Turn(pool, s_self["pool"])

            def rstd_of(kind, c):
                i = NORMS.index((kind, c))
                pool.wait_ge(S["stats"], i + 1)
                me.step(g.tensor_scalar(rs[:, i, :], mv[:, i, :, 1], LN_EPS, None, ALU.add))
                g.tensor_tensor(rs[:, i, :], rs[:, i, :], half_down[:], ALU.pow).then_inc(S["rstd"], 1)

            me.step(g.memset(half_down[:], -0.5))
            rstd_of("a_in", 0)
            rstd_of("a_in", 1)
            for c in range(CHUNKS):
                if c + 2 < CHUNKS:
                    rstd_of("a_in", c + 2)
                b, half = divmod(c, 2)
                at = slice(half * CHUNK, (half + 1) * CHUNK)
                for i, (dst, r1, r2, summed) in enumerate(((q_t, "rq1", "rq2", "ropeq"), (k_t, "rk1", "rk2", "ropek"))):
                    pool.wait_ge(S[r1], c + 1)
                    pool.wait_ge(S[r2], c + 1)
                    g.tensor_tensor(dst[:, b, at], dst[:, b, at], rot[:, i, :], ALU.add).then_inc(S[summed], 1)
            for t in (u_q, u_k):
                me.step(g.memset(t[:].rearrange("p a b c -> p (a b c)"), 0.0))
            me.step(g.memset(v_h[:].rearrange("p a b c -> p (a b c)"), 0.0))
            me.step(g.memset(v_h[:, :, :, VH:VH + 1].rearrange("p a b c -> p (a b) c"), 1.0))
            for i in range(4, 9):
                rstd_of(*NORMS[i])

            def squares(c):
                pool.wait_ge(S["raw_c"], CT * (c + 1))
                if c:
                    pool.wait_ge(S["lo_c"], c)
                g.tensor_tensor(sq[:], raw[:], raw[:], ALU.mult).then_inc(S["sq_c"], 1)

            q_parts = (0, 0, 1, 0, 2, 1)
            k_parts = (0, 1, 0, 2, 0, 1)

            def spread(dst, which, parts, n, done):
                for seg, i in enumerate(parts):
                    out_ap = dst[:, n % 2].rearrange("p t (c r) -> p t c r", c=2)[:, :, :, seg * DH:(seg + 1) * DH]
                    in_ap = part[i][:, which, n, :].rearrange("p (t c d) -> p t c d", t=BT, c=2)
                    last = g.tensor_scalar(out_ap, in_ap, 1.0, None, ALU.mult)
                last.then_inc(S[done], 1)

            def build_qk(n):
                if n >= 2:
                    pool.wait_ge(S["turned"], turns_done(("k", n - 2)))
                spread(u_k, 1, k_parts, n, "uk")
                if n >= 2:
                    pool.wait_ge(S["turned"], turns_done(("q", n - 2)))
                spread(u_q, 0, q_parts, n, "uq")

            def build_v(n):
                u = n % 2
                if n >= 2:
                    pool.wait_ge(S["g"], BT * (n - 1))
                g.tensor_scalar(gain[:, u:u + 1], gains[:, n:n + 1], 1.0, None, ALU.mult).then_inc(S["gcp"], 1)
                if n >= 2:
                    pool.wait_ge(S["av"], BT * (n - 1))
                g.tensor_scalar(v_h[:, u, :, 0:VH], v_c[:, n, :, :], 1.0, None, ALU.mult).then_inc(S["vh"], 1)

            rstd_of("b_in", 1)
            pool.wait_ge(ld["cw"], 64)
            for b in range(BATCH):
                me.step(g.tensor_scalar(gains[:, b * HEADS:(b + 1) * HEADS], sm[:, SM_GAIN:SM_GAIN + HEADS],
                                        1.0, None, ALU.mult))
            for c in range(1, CHUNKS):
                rstd_of("b_out", c - 1)
                if c + 1 < CHUNKS:
                    rstd_of("b_in", c + 1)
                rstd_of("c_in", c - 1)
                if c == CHUNKS - 1:
                    pool.wait_ge(S["lo_c"], 2)
                    pool.wait_ge(S["vraw_c"], 2 * CT)
                    build_qk(0)
                    build_v(0)
                squares(c - 1)
            build_qk(1)
            build_v(1)

            def parts(c):
                pool.wait_ge(S["rs_c"], c - CHUNKS + 3)
                me.step(g.tensor_tensor(sq[:].rearrange("p a h (g d) -> p (a h g) d", d=DH),
                                        raw[:].rearrange("p a h (g d) -> p (a h g) d", d=DH),
                                        rstd[:].unsqueeze(2).to_broadcast([P, P, DH]), ALU.mult))
                at = part_at(c)
                me.step(g.tensor_scalar(part[0][at], sq[:], 1.0, None, ALU.mult))
                me.step(g.tensor_tensor(raw[:], sq[:], part[0][at], ALU.subtract))
                me.step(g.tensor_scalar(part[1][at], raw[:], 1.0, None, ALU.mult))
                g.tensor_tensor(part[2][at], raw[:], part[1][at], ALU.subtract).then_inc(S["lo_c"], 1)

            rstd_of("b_out", CHUNKS - 1)
            rstd_of("c_in", CHUNKS - 1)
            parts(CHUNKS - 2)

            def heads_a(b):
                pool.wait_ge(S["ro"], b + 1)
                o = o_all[:, b * HEADS:(b + 1) * HEADS, :, :, :].rearrange("p h c g v -> p (h c) g v")
                if b:
                    pool.wait_ge(S["yc"], 2)
                for half in range(2):
                    for comp in range(2):
                        last = g.tensor_tensor(t_o[half][:, comp], o[:, :, 2 * comp + half, 0:VH],
                                               r_o[:, half, comp, :].unsqueeze(2).to_broadcast([P, HEADS * CT, VH]),
                                               ALU.mult)
                    me.step(last)
                    me.step(g.tensor_tensor(t_o[half][:, 0], t_o[half][:, 0], t_o[half][:, 1], ALU.add))
                    g.tensor_tensor(t_o[half][:, 1], t_o[half][:, 0], t_o[half][:, 0],
                                    ALU.mult).then_inc(S["to_a"], 1)

            def heads_b(b):
                pool.wait_ge(S["ms_o"], b + 1)
                for half in range(2):
                    c = 2 * b + half
                    if b:
                        pool.wait_ge(S["turned"], turns_done(("y", half)))
                    out_ap = y_c[half][:].rearrange("p c (h v) -> p h c v", h=HEADS)
                    in_ap = t_o[half][:, 0].rearrange("p (h c) v -> p h c v", h=HEADS)
                    r_ap = rstd[:, half * HEADS * CT:(half + 1) * HEADS * CT].rearrange(
                        "p (h c) -> p h c", h=HEADS).unsqueeze(3).to_broadcast([P, HEADS, CT, VH])
                    g.tensor_tensor(out_ap, in_ap, r_ap, ALU.mult).then_inc(S["yc"], 1)

            late = CHUNKS - 1
            for n in range(2, NH + 1):
                if n < NH:
                    if n == HEADS:
                        pool.wait_ge(S["lo_c"], CHUNKS)
                        pool.wait_ge(S["turn_read"], turns_done(("late qkv", CT - 1)))
                    build_qk(n)
                if n == 6:
                    squares(late)
                if n == 7:
                    parts(late)
                if n == 11:
                    heads_a(0)
                if n == 12:
                    heads_b(0)
                if n == 14:
                    rstd_of("c_out", 0)
                if n == 15:
                    rstd_of("d_in", 0)
                if n < NH:
                    build_v(n)
            rstd_of("c_out", 1)
            rstd_of("d_in", 1)
            heads_a(1)

            for c in range(CHUNKS):
                for e in range(EXPERTS):
                    n = EXPERTS * c + e
                    pool.wait_ge(S["sc_d"], n + 1)
                    if e == 0:
                        if c >= 2:
                            pool.wait_ge(S["xfin"], c - 1)
                        g.tensor_scalar(y_d(c), e_out[:, 0], 1.0, None, ALU.mult).then_inc(S["ad_d"], 1)
                    else:
                        pool.wait_ge(S["ad_d"], n)
                        g.tensor_tensor(y_d(c), y_d(c), e_out[:, e % 2], ALU.add).then_inc(S["ad_d"], 1)
                    at = (c, e)
                    if at == (0, 2):
                        heads_b(1)
                    if at == (0, 7):
                        rstd_of("c_out", 2)
                    if at == (1, 0):
                        rstd_of("d_out", 0)
                    if at == (1, 1):
                        rstd_of("d_in", 2)
                        rstd_of("c_out", 3)
                    if at == (1, 3):
                        rstd_of("d_in", 3)
                    if c >= 2 and e == 0:
                        rstd_of("d_out", c - 1)
            rstd_of("d_out", CHUNKS - 1)


_OUTS = (BATCH, SEQ, P)


def kernel(**inputs):
    import ml_dtypes
    import numpy as _np
    import concourse.bacc as _bacc
    from concourse import mybir as _mybir
    from concourse.bass_utils import run_bass_kernel_spmd as _run

    f = {k: _np.asarray(v) for k, v in inputs.items()}

    order = _np.concatenate([_np.arange(0, P, 2), _np.arange(1, P, 2)])
    swapped = _np.concatenate([order[P // 2:], order[:P // 2]])
    wq, wk, wv = f["L0_attn_Wq"], f["L0_attn_Wk"], f["L0_attn_Wv"]
    a_w = _np.concatenate([wq[order].T, wq[swapped].T, wk[order].T, wk[swapped].T, wv.T], axis=1)
    b_w12 = _np.concatenate([f["L0_ffn_w1_w"].T, f["L0_ffn_w2_w"].T], axis=1)

    def by_k(w):
        return w.T.reshape(-1, P, w.shape[0]).transpose(1, 0, 2)

    def cols(s):
        return s.reshape(-1, P).T

    def rows(s):
        return _np.broadcast_to(s.reshape(1, -1), (P, s.size))

    b_s = _np.concatenate([cols(f[f"L0_ffn_{n}_s"]) for n in ("w1", "w2", "h1", "h2")], axis=1)
    c_w = _np.concatenate([f["L1_attn_Wq"].T, f["L1_attn_Wk"].T, f["L1_attn_Wv"].T], axis=1)
    small = _np.concatenate([rows(f["L1_attn_" + n]) for n in (
        "lambda_q1", "lambda_k1", "lambda_q2", "lambda_k2", "delta_gain", "cos_head_delta",
        "cos_logit_scale_raw")] + [rows(f["L1_ffn_temperature"]), _np.tile(f["L1_attn_subln_weight"], HEADS)[:, None],
        (_np.arange(P)[:, None] // (P // 2) == _np.arange(2)[None, :]).astype(_np.float32)], axis=1)

    theta = (_np.float32(10000.0) ** (_np.float32(-2.0) * _np.arange(P // 2, dtype=_np.float32) / _np.float32(P))).astype(_np.float32)
    ang = (_np.arange(SEQ, dtype=_np.float32)[:, None] * theta[None, :]).astype(_np.float32).T
    cos, sin = _np.cos(ang), _np.sin(ang)
    rope = _np.stack([_np.concatenate([cos, cos]), _np.concatenate([-sin, sin])], axis=1).astype(_np.float32)
    eye = _np.eye(P, dtype=_np.float32)
    mask = _np.where(_np.arange(P + 1)[None, :] <= _np.arange(P)[:, None] + 1, 0.0, MASKED).astype(ml_dtypes.bfloat16)
    before = (_np.arange(EXPERTS)[None, :] < _np.arange(EXPERTS)[:, None]).astype(_np.float32)
    before = _np.broadcast_to(before.reshape(1, -1), (P, EXPERTS * EXPERTS))

    arrays = {
        "x": f["L0_attn_x"], "a_w": a_w, "rope": rope, "b_w12": b_w12, "b_h1": by_k(f["L0_ffn_h1_w"]),
        "b_h2": by_k(f["L0_ffn_h2_w"]), "b_w3": by_k(f["L0_ffn_w3_w"]), "b_s": b_s,
        "b_s3": rows(f["L0_ffn_w3_s"]), "c_w": c_w, "c_wo": f["L1_attn_Wo"].T, "c_bo": rows(f["L1_attn_bo"]),
        "small": small, "d_wg": f["L1_ffn_Wg"].transpose(1, 0, 2), "d_wu": f["L1_ffn_Wu"].transpose(1, 0, 2),
        "d_wd": f["L1_ffn_Wd"].transpose(1, 0, 2), "d_wr": f["L1_ffn_Wr"], "ident": eye,
        "ident_bf": eye.astype(ml_dtypes.bfloat16), "mask": mask, "before": before,
    }
    nc = _bacc.Bacc("TRN2", target_bir_lowering=False, num_devices=1)
    feed, args = {}, []
    for name, a in arrays.items():
        a = _np.ascontiguousarray(a)
        feed[f"in_{name}"] = a
        args.append(nc.dram_tensor(f"in_{name}", a.shape, _mybir.dt.from_np(a.dtype), kind="ExternalInput").ap())
    args.append(nc.dram_tensor("out_0", _OUTS, F32, kind="ExternalOutput").ap())
    sandwich(nc, *args)
    r = _run(nc, [feed], core_ids=[0])
    return r.results[0]["out_0"]
```
